# Optimizing a Trainium2 kernel written in Bass

```python
import numpy as np
import jax
import jax.numpy as jnp

def _softmax(x, axis=-1):
    return jax.nn.softmax(x, axis=axis)

def _gelu(x):
    return jax.nn.gelu(x, approximate=True)

def _silu(x):
    return jax.nn.silu(x)

def _sigmoid(x):
    return jax.nn.sigmoid(x)

def _layernorm(x, axis=-1, eps=1e-05):
    m = jnp.mean(x, axis=axis, keepdims=True)
    v = jnp.var(x, axis=axis, keepdims=True)
    return (x - m) / jnp.sqrt(v + eps)

def _scatter_add(tgt, idx, src, axis=0):
    return tgt.at[idx].add(src)

def _segment_sum(src, seg, n):
    return jax.ops.segment_sum(src, seg, n)
kernel_name = 'mk_adaln_d1_jaxref_r8_3e5533'

def setup_inputs(seed: int=0):
    np.random.seed(seed)
    _w = jnp.asarray

    def _L0_attn_setup():
        import jax, jax.numpy as jnp
        import numpy as np
        B, N, D = (2, 256, 128)
        H, FD, HD = (16, 16, 64)
        ENC = 64
        EPS = 1e-12
        RD = 4.0
        RRD = 2.0
        R2 = float(np.sqrt(2.0))

        def taylor_exp(x):
            x2 = (x[..., :, None] * x[..., None, :]).reshape(*x.shape[:-1], FD * FD) / R2
            return jnp.concatenate([jnp.ones_like(x[..., :1]), x / RRD, x2 / RD], axis=-1)
        key = jax.random.key(seed)
        ks = jax.random.split(key, 7)
        s = 1.0 / np.sqrt(D)
        x = jax.random.normal(ks[0], (B, N, D), dtype=jnp.float32)
        Wq = jax.random.normal(ks[1], (H * FD, D), dtype=jnp.float32) * s
        Wk = jax.random.normal(ks[2], (H * FD, D), dtype=jnp.float32) * s
        Wv = jax.random.normal(ks[3], (H * HD, D), dtype=jnp.float32) * s
        Wk_enc = jax.random.normal(ks[4], (H * FD, D), dtype=jnp.float32) * s
        Wv_enc = jax.random.normal(ks[5], (H * HD, D), dtype=jnp.float32) * s
        Wout = jax.random.normal(ks[6], (D, H * HD), dtype=jnp.float32) * s
        return {'x': x, 'Wq': Wq, 'Wk': Wk, 'Wv': Wv, 'Wk_enc': Wk_enc, 'Wv_enc': Wv_enc, 'Wout': Wout}
    _L0_attn_in = _L0_attn_setup()

    def _L0_ffn_setup():
        import jax, jax.numpy as jnp
        import numpy as np
        E = 8
        K = 2
        D = 128
        P = 512
        key = jax.random.key(seed)
        ks = jax.random.split(key, 8)
        s = lambda fan_in: 1.0 / np.sqrt(fan_in)
        x = jax.random.normal(ks[0], (2, 256, D), dtype=jnp.float32)
        W1 = jax.random.normal(ks[1], (E, D, P), dtype=jnp.float32) * s(D)
        b1 = jax.random.normal(ks[2], (E, P), dtype=jnp.float32) * 0.01
        W2 = jax.random.normal(ks[3], (E, P, D), dtype=jnp.float32) * s(P)
        b2 = jax.random.normal(ks[4], (E, D), dtype=jnp.float32) * 0.01
        Wr = jax.random.normal(ks[5], (D, E), dtype=jnp.float32) * s(D)
        br = jax.random.normal(ks[6], (E,), dtype=jnp.float32) * 0.01
        return {'x': x, 'W1': W1, 'b1': b1, 'W2': W2, 'b2': b2, 'Wr': Wr, 'br': br}
    _L0_ffn_in = _L0_ffn_setup()
    _L0_c = _w((lambda *s: np.random.randn(*s).astype(np.float32) * 0.05)(2, 128))
    _L0_wmod = _w((lambda *s: np.random.randn(*s).astype(np.float32) * 0.05)(128, 6 * 128) * 128 ** (-0.5))
    _d = {'L0_attn_x': _L0_attn_in['x'], 'L0_attn_Wq': _L0_attn_in['Wq'], 'L0_attn_Wk': _L0_attn_in['Wk'], 'L0_attn_Wv': _L0_attn_in['Wv'], 'L0_attn_Wk_enc': _L0_attn_in['Wk_enc'], 'L0_attn_Wv_enc': _L0_attn_in['Wv_enc'], 'L0_attn_Wout': _L0_attn_in['Wout'], 'L0_ffn_W1': _L0_ffn_in['W1'], 'L0_ffn_b1': _L0_ffn_in['b1'], 'L0_ffn_W2': _L0_ffn_in['W2'], 'L0_ffn_b2': _L0_ffn_in['b2'], 'L0_ffn_Wr': _L0_ffn_in['Wr'], 'L0_ffn_br': _L0_ffn_in['br'], 'L0_c': _L0_c, 'L0_wmod': _L0_wmod}
    _x0 = _d['L0_attn_x']
    _d['L0_attn_x'] = jax.random.normal(jax.random.fold_in(jax.random.key(seed), 1), (2, 1024, 128), dtype=_x0.dtype)
    del _x0
    return _d

def reference(L0_attn_x, L0_attn_Wq, L0_attn_Wk, L0_attn_Wv, L0_attn_Wk_enc, L0_attn_Wv_enc, L0_attn_Wout, L0_ffn_W1, L0_ffn_b1, L0_ffn_W2, L0_ffn_b2, L0_ffn_Wr, L0_ffn_br, L0_c, L0_wmod):

    def _L0_attn_ref(x, Wq, Wk, Wv, Wk_enc, Wv_enc, Wout):
        import jax, jax.numpy as jnp
        import numpy as np
        B, N, D = (2, 256, 128)
        H, FD, HD = (16, 16, 64)
        ENC = 64
        EPS = 1e-12
        RD = 4.0
        RRD = 2.0
        R2 = float(np.sqrt(2.0))

        def taylor_exp(x):
            x2 = (x[..., :, None] * x[..., None, :]).reshape(*x.shape[:-1], FD * FD) / R2
            return jnp.concatenate([jnp.ones_like(x[..., :1]), x / RRD, x2 / RD], axis=-1)
        b, n, _ = x.shape
        q = (x @ Wq.T).reshape(b, n, H, FD).transpose(0, 2, 1, 3)
        k = (x @ Wk.T).reshape(b, n, H, FD).transpose(0, 2, 1, 3)
        v = (x @ Wv.T).reshape(b, n, H, HD).transpose(0, 2, 1, 3)
        x_enc = x[:, :ENC]
        k_enc = (x_enc @ Wk_enc.T).reshape(b, ENC, H, FD).transpose(0, 2, 1, 3)
        v_enc = (x_enc @ Wv_enc.T).reshape(b, ENC, H, HD).transpose(0, 2, 1, 3)
        k_enc_f = taylor_exp(k_enc)
        q_f = taylor_exp(q)
        k_f = taylor_exp(k)
        A_qk = jnp.einsum('bhnd,bhmd->bhnm', q_f, k_f)
        A_qk = jnp.tril(A_qk)
        y1 = jnp.einsum('bhnm,bhme->bhne', A_qk, v)
        A_qk2 = jnp.einsum('bhnd,bhmd->bhnm', q_f, k_enc_f)
        y2 = jnp.einsum('bhnm,bhme->bhne', A_qk2, v_enc)
        k_state = k_enc_f.sum(axis=2, keepdims=True) + jnp.cumsum(k_f, axis=2)
        z = 1.0 / ((q_f * k_state).sum(axis=-1) + EPS)
        out = (y1 + y2) * z[..., None]
        out = out.transpose(0, 2, 1, 3).reshape(b, n, H * HD)
        return out @ Wout.T

    def _L0_ffn_ref(x, W1, b1, W2, b2, Wr, br):
        import jax, jax.numpy as jnp
        import numpy as np
        E = 8
        K = 2
        D = 128
        P = 512
        B, S, _ = x.shape
        xf = x.reshape(B * S, D)
        scores = xf @ Wr + br
        _, top_idx = jax.lax.top_k(scores, K)
        mask = jax.nn.one_hot(top_idx, E, dtype=scores.dtype).sum(-2) > 0
        router_weights = jax.nn.softmax(jnp.where(mask, scores, -jnp.inf), axis=-1)
        h = jax.nn.gelu(jnp.einsum('td,edp->etp', xf, W1) + b1[:, None, :])
        y = jnp.einsum('etp,epd->etd', h, W2) + b2[:, None, :]
        out = jnp.einsum('te,etd->td', router_weights, y)
        return out.reshape(B, S, D)
    x = L0_attn_x
    mod = (_silu(L0_c) @ L0_wmod).reshape(L0_c.shape[0], 6, 1, -1)
    sa, ca, ga, sb, cb, gb = (mod[:, 0], mod[:, 1], mod[:, 2], mod[:, 3], mod[:, 4], mod[:, 5])
    ga = (2 * (ga >= 0) - 1) * jnp.maximum(jnp.abs(ga), 0.25)
    gb = (2 * (gb >= 0) - 1) * jnp.maximum(jnp.abs(gb), 0.25)
    h = _layernorm(x, axis=-1) * (1 + ca) + sa
    x = x + ga * _L0_attn_ref(h, L0_attn_Wq, L0_attn_Wk, L0_attn_Wv, L0_attn_Wk_enc, L0_attn_Wv_enc, L0_attn_Wout)
    h = _layernorm(x, axis=-1) * (1 + cb) + sb
    x = x + gb * _L0_ffn_ref(h, L0_ffn_W1, L0_ffn_b1, L0_ffn_W2, L0_ffn_b2, L0_ffn_Wr, L0_ffn_br)
    return x

_drawn_inputs = setup_inputs


def setup_inputs(seed=0):
    import zlib

    import numpy as np

    out = dict(_drawn_inputs(seed))
    spreads = {}
    factors = {'L0_ffn_b1': 44.55, 'L0_ffn_b2': 31.04, 'L0_ffn_br': 6.345}
    for name, (base, spread) in spreads.items():
        noise = np.random.default_rng([zlib.crc32(name.encode()), seed]).standard_normal(out[name].shape)
        drawn = base * np.exp(spread * noise) if base else spread * noise
        out[name] = jnp.asarray(drawn.astype(out[name].dtype))
    for name, factor in factors.items():
        out[name] = (out[name] * factor).astype(out[name].dtype)
    return out
```

```python
from contextlib import ExitStack

import concourse.bass as bass
from concourse import mybir

F32 = mybir.dt.float32
F16 = mybir.dt.float16
BF16 = mybir.dt.bfloat16
ACT = mybir.ActivationFunctionType
ALU = mybir.AluOpType
AX = mybir.AxisListType

P = 128
B, N, D = 2, 1024, 128
H, FD, HD = 16, 16, 64
ENC = 64
E, PF = 8, 512
PT = PF // P
TILES = B * N // P
BT = N // P
PAIRS = H // 2
NP = B * PAIRS
CH = 4
CT = TILES // CH
VW = 130
VROW = 2 * (BT + 1) * VW
EPS = 1e-12
LN_EPS = 1e-5
SQ_SCALE = 0.25 * 2.0 ** -0.5
SQ_BIAS = 2.0 ** -0.5
A_BUFS = 4
S_BUFS = 2
LAG = 3

def _units():
    first = lambda s: [(0, 512, s, 0, 0), (512, 384, s, 1, 128), (896, 128, s, 3, 384)]
    full = lambda s, j: [(0, 512, s, j, 512), (512, 512, s, j + 1, 512)]
    last = lambda s: [(0, 512, s, 4, 512), (512, 384, s, 5, 640), (896, 128, s, 7, 896)]
    mid = [(0, 256, 0, 2, 256), (256, 256, 0, 6, 768), (512, 256, 1, 2, 256), (768, 256, 1, 6, 768)]
    enc = [(0, 512, None, "enc", 0), (512, 512, None, "enc", 512)]
    return [enc, first(0), first(1), mid, full(0, 0), full(0, 2), last(0), full(1, 0), full(1, 2), last(1)]


UNITS = _units()
NU = len(UNITS)
MASKED = (1, 2, 3, 6, 9)
DONE_AFTER = {3: [(0, 0), (1, 0)], 6: [(0, 1)], 9: [(1, 1)]}
GROUPS = [(0, 0), (1, 0), (0, 1), (1, 1)]


def adaln_block(nc, x, wqkT, wvT, woT, w1, b1T, w2, b2, wr, br, cT, wmod, ident, half_count, before, out):
    ctx = ExitStack()
    with ctx:
        def sb(name, shape, dt):
            return ctx.enter_context(nc.sbuf_tensor(name, shape, dt))

        def sem(name):
            return ctx.enter_context(nc.semaphore(name))

        xs = sb("xs", [P, TILES, D], F32)
        hTf = sb("hTf", [P, TILES * P], F32)
        hh = sb("hh", [P, TILES * P], F16)
        hl = sb("hl", [P, TILES * P], F16)
        ch = sb("ch", [P, TILES * P], F16)
        cl = sb("cl", [P, TILES * P], F16)
        WA = 3 * 256 + 3 * 1024
        wah = sb("wah", [P, WA], F16)
        wal = sb("wal", [P, WA], F16)
        Q0, K0, KE0, V0, VE0, O0 = 0, 256, 512, 768, 768 + 1024, 768 + 2048
        w1h = sb("w1h", [P, E, PF], F16)
        w1l = sb("w1l", [P, E, PF], F16)
        w2h = sb("w2h", [P, E, PT, D], F16)
        w2l = sb("w2l", [P, E, PT, D], F16)
        C = sb("C", [P, NP, BT, 2, HD + 1], F32)
        vst = sb("vst", [P, 2, PAIRS, 2 * VW], F16)
        id32 = sb("id32", [P, P], F32)
        arena = sb("arena", [P, 49152 // 4], F32)

        def view(byte, shape, dt):
            n = 1
            for s in shape:
                n *= s
            size = n * (4 if dt == F32 else 2)
            a = arena[:, byte // 4:(byte + size) // 4]
            if dt != F32:
                a = a.bitcast(dt)
            if len(shape) > 1:
                names = "abcd"[:len(shape)]
                a = a.rearrange(f"p ({' '.join(names)}) -> p {' '.join(names)}",
                                **{n_: s for n_, s in zip(names, shape)})
            return a

        xn = view(0, [TILES, D], F32)
        wst = view(8192, [WA], F32)
        wms = view(8192 + WA * 4, [6 * D], F32)
        cums = view(8192 + WA * 4 + 6 * D * 4, [N], F32)
        ffs = view(32768, [E * PF], F32)
        plain = {n_: view(8192 * i, [B, 2, N], F16) for i, n_ in enumerate(("qh", "ql", "kh", "kl"))}
        A32 = [view(4096 * i, [1024], F32) for i in range(A_BUFS)]
        Alo = [view(16384 + 2048 * i, [1024], F16) for i in range(A_BUFS)]
        SLOT = 2 * (N + 2 * N + P + VROW)
        SLOT0 = 49152 - 1024 - 2 * SLOT
        qS = [view(SLOT0 + SLOT * i, [N], F16) for i in range(2)]
        kS = [view(SLOT0 + SLOT * i + 2 * N, [2 * N + P], F16) for i in range(2)]
        vS = [view(SLOT0 + SLOT * i + 2 * (3 * N + P), [VROW], F16) for i in range(2)]
        an = [view(4096 * i, [H, HD], F32) for i in range(2)]
        aTh = [view(8192 + 2048 * i, [PAIRS, P], F16) for i in range(2)]
        aTl = [view(12288 + 2048 * i, [PAIRS, P], F16) for i in range(2)]
        tmp = [view(16384 + 512 * i, [D], F32) for i in range(2)]
        xn2 = view(24576, [TILES, D], F32)
        G = [view(8192 * i, [PT, 512], F32) for i in range(2)]
        Glo = [view(16384 + 4096 * i, [PT, 512], F16) for i in range(2)]
        acc = view(32768, [TILES, D], F32)

        kenc_sb = hTf[:, 0:N].bitcast(F16).rearrange("p (b c s g t) -> p b c s g t", b=B, c=2, s=2, g=2)
        kenc = [[[kenc_sb[:, b, part, s] for s in range(2)] for part in range(2)] for b in range(B)]
        vencst = sb("vencst", [P, B, PAIRS, VW], F16)
        stats = view(31744, [TILES, 6], F32)
        mv = sb("mv", [P, TILES, 2], F32)
        rs = sb("rs", [P, 4, TILES], F32)
        cs = sb("cs", [P, B], F32)
        scT = sb("scT", [P, B], F32)
        scb = view(30720, [B, P], F32)
        modT = sb("modT", [P, 4, B], F32)
        gate = sb("gate", [P, 4, P], F32)
        gtmp = view(8192 + WA * 4 + 6 * D * 4, [4, P], F32)
        hc = sb("hc", [P, BT], F32)
        sqb = sb("sqb", [P, 1], F32)
        zr = view(18432, [NP, BT, 2], F32)
        wrs = sb("wrs", [P, E], F32)
        brs = sb("brs", [P, E], F32)
        bef = view(48640, [E, E], F32)
        b1s = sb("b1s", [P, E, PT], F32)
        b2s = view(48128, [D], F32)
        sco = view(0, [TILES, E], F32)
        rk = view(512, [TILES, E], F32)
        cmp2 = arena[:, 4096:4096 + 2048].rearrange("p (a b c) -> p a b c", a=2 * TILES, b=E)
        mx = sb("mx", [P, TILES], F32)
        wts = view(40960, [TILES, 32], F32)
        wT = view(43008, [4, P], F32)

        ps = ctx.enter_context(nc.psum_tensor("ps", [P, 8, 512], F32))
        Sb = [ps[:, 2 * i:2 * i + 2, :].rearrange("p a b -> p (a b)") for i in range(2)]

        sQ = nc.dram_tensor("scratch_q", [B, P, PAIRS, N], F16, kind="Internal").ap()
        sK = nc.dram_tensor("scratch_k", [B, P, PAIRS, N], F16, kind="Internal").ap()
        sKE = nc.dram_tensor("scratch_k_enc", [B, P, PAIRS, P], F16, kind="Internal").ap()
        sV = nc.dram_tensor("scratch_v", [NP, P, VROW], F16, kind="Internal").ap()

        ld_c = sem("c_loaded"); ld_x = [sem(f"x_loaded{q}") for q in range(CH)]; ld_wa = sem("attn_weights_loaded")
        ld_w1 = sem("w1_loaded"); ld_w2 = sem("w2_loaded"); ld_k = sem("consts_loaded"); ld_b2 = sem("b2_loaded")
        silu_done = sem("silu_done"); scb_done = sem("silu_broadcast")
        mod_ps = sem("mod_products"); mod_done = sem("mod_evacuated")
        gate_step = sem("gate_step"); gate_done = sem("gate_done")
        wa_hi = sem("wa_hi"); wa_lo = sem("wa_lo"); ff_split = sem("ffn_split")
        setup_done = sem("setup_done"); kenc_zero = sem("kenc_zeroed"); pool_turn = sem("pool_turn"); enc_stored = sem("encoder_stored"); slot_zeroed = sem("slots_zeroed")
        st_done = sem("bn_stats_done"); agg_done = sem("bn_aggr_done")
        var_done = sem("var_plus_eps"); std_done = sem("std_done"); rstd_step = sem("rstd_step")
        xn_done = sem("xn_done"); tr_done = sem("transposed"); hTf_done = sem("hTf_done")
        hh_done = sem("hh_done"); hl_done = sem("hl_done")
        scan_done = sem("scan_done"); chi_done = sem("cum_hi"); clo_done = sem("cum_lo")
        prj_ps = sem("projection_products"); prj_hi = sem("projection_hi"); prj_out = sem("projection_out")
        prj_free = sem("projection_bank_free")
        v_stored = [sem("v_stored_even"), sem("v_stored_odd")]; stacked = [sem("stacked_batch0"), sem("stacked_batch1")]
        enc_ps = sem("enc_products"); enc_hi = sem("enc_hi"); enc_lo = sem("enc_lo")
        slot = [sem("slot0_loaded"), sem("slot1_loaded")]
        s_ready = sem("scores_ready");
        sq_done = sem("squared"); mk_done = sem("masked"); lo_done = sem("a_lo_done")
        av_done = sem("a_buffers_free_and_units_done")
        y_free = sem("y_bank_free")
        z_done = sem("z_done"); an_done = sem("normalized"); at_ps = sem("attn_transposed")
        at_hi = sem("attnT_hi"); at_lo = sem("attnT_lo"); o_ps = sem("out_products"); g_done = sem("gated")
        x1_done = sem("x1_done")
        sc_ps = sem("router_products"); rt = sem("router_step"); exp_done = sem("exp_done")
        w_ready = sem("expert_weights_ready"); wt_ps = sem("weights_transposed"); wt_done = sem("wT_done")
        up_ps = sem("up_products"); g_ok = sem("gelu_done"); glo = sem("gelu_lo"); up_free = sem("g_buffer_free")
        dn_ps = sem("down_products"); acc_done = sem("accumulated"); b2_ps = sem("b2_products")
        fin_done = sem("final_done"); out_done = sem("out_stored"); fstep = sem("final_step")

        prj_c = sem("running_sums_out"); count_done = sem("half_counts_in_C"); chain = sem("vector_chain"); z0 = sem("den_ready"); dn_free = sem("down_bank_free")
        TOTAL_PRJ = 5 * 4

        def part_at(name, c, g):
            return plain[name][:, bass.ds(c // 2, 1), g, bass.ds((c % 2) * 512, 512)].rearrange("p a t -> p (a t)")

        def sums_at(c, i, half):
            at = C[:, bass.ds((c // 2) * PAIRS + 4 * half, 4), bass.ds((c % 2) * CT + i, 1), :, 0:HD]
            return at.rearrange("p n a s e -> p (n a) s e")

        block = ctx.enter_context(nc.Block())

        @block.sync
        def _(sp):
            sp.dma_start(cs[:], cT).then_inc(ld_c, 16)
            sp.dma_start(wms, wmod).then_inc(ld_c, 16)
            for q in range(4):
                sp.dma_start(xs[:, CT * q:CT * q + CT, :],
                             x[CT * q:CT * q + CT].rearrange("t p d -> p t d")).then_inc(ld_x[q], 16)
            sp.dma_start(id32[:], ident).then_inc(ld_k, 16)
            sp.dma_start(wst[:, 0:V0], wqkT).then_inc(ld_wa, 16)
            sp.dma_start(wst[:, V0:O0], wvT).then_inc(ld_wa, 16)
            sp.dma_start(wst[:, O0:WA], woT).then_inc(ld_wa, 16)
            sp.dma_start(ffs, w1).then_inc(ld_w1, 16)
            for dst, src in ((hc[:], half_count), (wrs[:], wr), (b1s[:], b1T)):
                sp.dma_start(dst, src).then_inc(ld_k, 16)
            sp.dma_start(brs[:], br.partition_broadcast(P)).then_inc(ld_k, 16)
            sp.wait_ge(ff_split, 2)
            sp.dma_start(ffs, w2).then_inc(ld_w2, 16)
            def store_v(c):
                for i in range(CT):
                    sp.wait_ge(prj_out, 12 * c + 4 + 2 * (i + 1))
                    b, t = c // 2, CT * (c % 2) + i
                    sp.dma_start(sV[PAIRS * b:PAIRS * (b + 1), :, 2 * VW * t:2 * VW * (t + 1)].rearrange("n p v -> p n v"),
                                 vst[:, i % 2]).then_inc(v_stored[i % 2], 16)

            def store_encoder(b):
                sp.wait_ge(enc_lo, 2 * b + 1)
                for part, rows in ((0, (0, 1)), (1, (2, 3))):
                    for s in range(2):
                        for r in rows:
                            to = sKE[b, 64 * s + 16 * r:64 * s + 16 * r + 16].rearrange("i (k g) t -> k i (g t)", g=2)
                            sp.dma_start(to, kenc[b][part][s][64 * s:64 * s + 64].rearrange("p g t -> p (g t)"))\
                              .then_inc(enc_stored, 16)
                sp.wait_ge(enc_lo, 2 * b + 2)
                for s in range(2):
                    rows, col = slice(64 * s, 64 * s + 64), VW * (2 * BT + s)
                    sp.dma_start(sV[PAIRS * b:PAIRS * (b + 1), rows, col:col + VW].rearrange("n p v -> p n v"),
                                 vencst[rows, b]).then_inc(enc_stored, 16)

            sp.sem_inc(v_stored[0], 16)
            sp.sem_inc(v_stored[1], 16)
            store_encoder(0)
            store_encoder(1)
            for c in range(CH):
                store_v(c)

            def load(n, hf):
                lo, hi, V2 = slice(0, 64), slice(64, P), 2 * VW * BT
                for dst, src, rows in ((qS[hf], sQ, slice(0, P)), (kS[hf][lo, 0:N], sK, lo), (kS[hf][hi, N:2 * N], sK, hi),
                                       (kS[hf][:, 2 * N:], sKE, slice(0, P))):
                    at = src[bass.ds(n // PAIRS, 1), rows, bass.ds(n % PAIRS, 1), :]
                    sp.dma_start(dst, at.rearrange("a p n t -> (a p) (n t)")).then_inc(slot[hf], 16)
                for rows, c0, c1 in ((slice(0, P), 0, V2), (lo, V2, V2 + VW), (hi, V2 + VW, V2 + 2 * VW)):
                    sp.dma_start(vS[hf][rows, c0:c1], sV[bass.ds(n, 1), rows, c0:c1].rearrange("a p t -> (a p) t"))\
                      .then_inc(slot[hf], 16)

            sp.wait_ge(enc_stored, 16 * B * (8 + 2))
            sp.wait_ge(slot_zeroed, 1)
            for hf in range(2):
                sp.wait_ge(v_stored[hf], 16 * (TILES // 2 + 1))
            for b in range(B):
                sp.wait_ge(stacked[b], 16 * 16)
            sp.wait_ge(ff_split, 4)
            load(0, 0)
            load(1, 1)
            sp.dma_start(bef, before).then_inc(ld_b2, 16)
            for q in range(4):
                sp.dma_start(b2s[32 * q:32 * q + E, :], b2).then_inc(ld_b2, 16)
            with sp.Fori(0, NP // 2 - 1) as it:
                for hf in range(2):
                    sp.wait_ge(av_done, it * (2 * NU) + (NU * (hf + 1) + A_BUFS))
                    load(it * 2 + (hf + 2), hf)
            with sp.Fori(0, CH) as c:
                sp.wait_ge(fin_done, c + 1)
                sp.dma_start(out[bass.ds(c * CT, CT)].rearrange("t p d -> p t d"), acc[:, bass.ds(c * CT, CT), :]).then_inc(out_done, 16)
            sp.wait_ge(out_done, 16 * CH)

        @block.gpsimd
        def _(gp):
            for hf in range(2):
                gp.memset(vst[:, hf].rearrange("p a (s v) -> p a s v", s=2)[:, :, :, HD:HD + 1], 1.0)
                gp.memset(vencst[:, hf, :, HD:HD + 1], 1.0)
                gp.memset(vencst[:, hf, :, VW - 1:VW], 0.0)
                gp.memset(vst[:, hf].rearrange("p a (s v) -> p a s v", s=2)[:, :, :, VW - 1:VW], 0.0)
            gp.memset(sqb[:], SQ_BIAS).then_inc(setup_done, 1)
            for n, (ready, hi, lo) in enumerate(((ld_w1, w1h[:].rearrange("p e f -> p (e f)"), w1l[:].rearrange("p e f -> p (e f)")),
                                                 (ld_w2, w2h[:].rearrange("p e a d -> p (e a d)"), w2l[:].rearrange("p e a d -> p (e a d)")))):
                gp.wait_ge(ready, 16)
                gp.tensor_scalar(hi, ffs, 1.0, 0.0, ALU.mult, ALU.add).then_inc(ff_split, 1)
                gp.wait_ge(ff_split, 2 * n + 1)
                gp.tensor_tensor(lo, ffs, hi, ALU.subtract).then_inc(ff_split, 1)

            gp.wait_ge(clo_done, B)
            gp.memset(hTf[:, 0:N], 0.0).then_inc(kenc_zero, 1)

            def store_stack(b):
                for name, dst, rows in (("qh", sQ, (0, 2)), ("ql", sQ, (1, 3)), ("kh", sK, (0, 1)), ("kl", sK, (2, 3))):
                    for s in range(2):
                        for r in rows:
                            to = dst[b, 64 * s + 16 * r:64 * s + 16 * r + 16].rearrange("i (k g) t -> k i (g t)", g=2)
                            gp.dma_start(to, plain[name][64 * s:64 * s + 64, b].rearrange("p g t -> p (g t)"))\
                              .then_inc(stacked[b], 16)

            for b in range(B):
                gp.wait_ge(prj_out, 12 * (2 * b + 1) + 4)
                store_stack(b)
            for b in range(B):
                gp.wait_ge(stacked[b], 16 * 16)
            for hf in range(2):
                gp.memset(kS[hf][64:P, 0:N], 0.0)
                gp.memset(kS[hf][0:64, N:2 * N], 0.0)
                gp.memset(vS[hf][64:P, 2 * VW * BT:2 * VW * BT + VW], 0.0)
                last = gp.memset(vS[hf][0:64, 2 * VW * BT + VW:VROW], 0.0)
            last.then_inc(slot_zeroed, 1)

            def tri(ap, blocks):
                return nc.gpsimd.affine_select(out=ap, in_=ap, compare_op=ALU.is_ge, fill=0.0, base=0,
                                               pattern=[[0, blocks], [1, P]], channel_multiplier=-1)

            def squared(it, k):
                gp.wait_ge(sq_done, it * (2 * NU) + (k + 1))
                gp.sem_inc(pool_turn, 1)

            with gp.Fori(0, NP // 2) as it:
                for k in range(2 * NU):
                    a = A32[k % A_BUFS]
                    kk = k % NU
                    if kk == 0:
                        squared(it, k)
                        gp.tensor_scalar(a, a, 1.0, 0.5, ALU.mult, ALU.add).then_inc(mk_done, 1)
                    elif kk == 3:
                        squared(it, k)
                        tri(a.rearrange("p (b c) -> p b c", b=4)[:, :, 0:P], 4).then_inc(mk_done, 1)
                    elif kk in MASKED:
                        squared(it, k)
                        tri(a.rearrange("p (b c) -> p b c", b=2)[:, :, 0:P], 2)
                        tri(a[:, 896:1024].rearrange("p (b c) -> p b c", b=1), 1).then_inc(mk_done, 1)

            gp.wait_ge(z_done, 1)
            with gp.Fori(0, BT) as t:
                for b in range(B):
                    src = C[:, PAIRS * b:PAIRS * (b + 1), bass.ds(t, 1), :, 0:HD].rearrange("p n a s e -> p (n a) s e")
                    zz = zr[:, PAIRS * b:PAIRS * (b + 1), bass.ds(t, 1), :].rearrange("p n a s -> p (n a) s")[:, :, :, None]\
                        .to_broadcast([P, PAIRS, 2, HD])
                    gp.wait_ge(at_ps, t * 2 + (b + 1))
                    gp.sem_inc(pool_turn, 1)
                    gp.tensor_tensor(an[b].rearrange("p (n s) e -> p n s e", s=2), src, zz, ALU.mult).then_inc(an_done, 1)

        @block.scalar
        def _(act):
            act.wait_ge(ld_c, 32)
            nc.scalar.activation(scT[:], cs[:], ACT.Silu).then_inc(silu_done, 1)

            def stddev(k):
                act.wait_ge(var_done, k)
                nc.scalar.activation(rs[:, 1, :], rs[:, 0, :], ACT.Sqrt).then_inc(std_done, 1)

            def hidden_hi(k):
                with act.Fori(0, CH) as c:
                    act.wait_ge(hTf_done, CH * k + c + 1)
                    nc.scalar.activation(hh[:, bass.ds(c * 512, 512)], hTf[:, bass.ds(c * 512, 512)], ACT.Copy).then_inc(hh_done, 1)

            stddev(1)
            act.wait_ge(ld_wa, 48)
            nc.scalar.activation(wah[:], wst, ACT.Copy).then_inc(wa_hi, 1)
            hidden_hi(0)
            for b in range(B):
                act.wait_ge(scan_done, b + 1)
                nc.scalar.activation(ch[:, N * b:N * b + N], cums, ACT.Copy, scale=0.5).then_inc(chi_done, 1)

            act.wait_ge(kenc_zero, 1)
            for b in range(B):
                act.wait_ge(enc_ps, 2 * b + 1)
                for s in range(2):
                    nc.scalar.activation(kenc_sb[:, b, 0, s, :, 64 * s:64 * s + 64],
                                         ps[:, 4, 0:128].rearrange("p (g t) -> p g t", g=2), ACT.Copy).then_inc(enc_hi, 1)
                act.wait_ge(enc_ps, 2 * b + 2)
                for s in range(2):
                    nc.scalar.activation(vencst[64 * s:64 * s + 64, b, :, 0:HD],
                                         ps[64 * s:64 * s + 64, 5, :].rearrange("p (a e) -> p a e", e=HD), ACT.Copy).then_inc(enc_hi, 1)

            act.wait_ge(setup_done, 1)
            act.wait_ge(clo_done, B)
            act.wait_ge(count_done, 1)
            act.sem_inc(prj_c, 8)
            with act.Fori(0, CH) as c:
                for u in range(TOTAL_PRJ):
                    act.wait_ge(prj_ps, c * TOTAL_PRJ + (u + 1))
                    bank = ps[:, u % 4, :]
                    if u < 4:
                        dst = part_at(("qh", "kh")[u // 2], c, u % 2)
                        nc.scalar.activation(dst, bank, ACT.Copy).then_inc(prj_hi, 1)
                    elif u < 12:
                        i, half = (u - 4) // 2, u % 2
                        if half == 0:
                            act.wait_ge(v_stored[i % 2], c * 32 + 16 * (i // 2 + 1))
                        dst = vst[:, i % 2, 4 * half:4 * half + 4].rearrange("p a (s v) -> p a s v", s=2)[:, :, :, 0:HD]
                        nc.scalar.activation(dst, bank.rearrange("p (a s e) -> p a s e", a=4, s=2), ACT.Copy).then_inc(prj_hi, 1)
                    else:
                        i, half = (u - 12) // 2, u % 2
                        nc.scalar.activation(sums_at(c, i, half), bank.rearrange("p (a s e) -> p a s e", a=4, s=2),
                                             ACT.Copy).then_inc(prj_c, 1)
            nc.scalar.preload_act_table(ACT.Square)
            with act.Fori(0, NP // 2) as it:
                for k in range(2 * NU):
                    act.wait_ge(s_ready, it * (2 * NU) + (k + 1))
                    act.wait_ge(av_done, it * (2 * NU) + (k + 1))
                    nc.scalar.activation(A32[k % A_BUFS], Sb[k % S_BUFS], ACT.Square, bias=sqb[:, 0:1],
                                         scale=SQ_SCALE).then_inc(sq_done, 1)
            with act.Fori(0, BT) as t:
                for b in range(B):
                    act.wait_ge(at_ps, t * 2 + (b + 1) + 2)
                    act.wait_ge(o_ps, t * 2 + (b + 1))
                    nc.scalar.activation(aTh[b].rearrange("p a t -> p (a t)"), Sb[b], ACT.Copy).then_inc(at_hi, 1)
            stddev(2)
            hidden_hi(1)
            act.wait_ge(rt, 1)
            nc.scalar.activation(rk.rearrange("p t e -> p (t e)"), rk.rearrange("p t e -> p (t e)"), ACT.Exp).then_inc(exp_done, 1)
            nc.scalar.preload_act_table(ACT.Gelu_apprx_tanh)
            act.wait_ge(acc_done, 1)
            act.sem_inc(g_ok, PT)
            with act.Fori(0, CH) as c:
                for e in range(E):
                    act.wait_ge(dn_ps, c * E + (e + 1))
                    for pt in range(PT):
                        act.wait_ge(up_ps, c * (E * PT) + (e * PT + pt + 1))
                        nc.scalar.activation(G[e % 2][:, pt, :], ps[:, pt, :], ACT.Gelu_apprx_tanh,
                                             bias=b1s[:, e, pt:pt + 1]).then_inc(g_ok, 1)

        @block.vector
        def _(v):
            step = [0]

            def link(ins):
                step[0] += 1
                ins.then_inc(chain, 1)
                v.wait_ge(chain, step[0])

            v.wait_ge(silu_done, 1)
            nc.vector.tensor_copy(scb, scT[:, :, None].to_broadcast([P, B, P])).then_inc(scb_done, 1)

            def statistics(k):
                if k == 0:
                    for t in range(TILES):
                        if t % CT == 0:
                            v.wait_ge(ld_x[t // CT], 16)
                        nc.vector.bn_stats(stats[:, t, :], xs[:, t, :]).then_inc(st_done, 1)
                for t in range(TILES):
                    v.wait_ge(st_done, TILES * k + t + 1)
                    nc.vector.bn_aggr(mv[:, t, :], stats[:, t, :]).then_inc(agg_done, 1)
                v.wait_ge(agg_done, TILES * (k + 1))
                nc.vector.tensor_scalar(rs[:, 0, :], mv[:, :, 1], LN_EPS, None, ALU.add).then_inc(var_done, 1)
                v.wait_ge(var_done, k + 1)
                v.wait_ge(std_done, k + 1)
                link(nc.vector.reciprocal(rs[:, 2, :], rs[:, 1, :]))
                link(nc.vector.tensor_tensor(rs[:, 3, :], rs[:, 2, :], rs[:, 2, :], ALU.mult))
                link(nc.vector.tensor_tensor(rs[:, 3, :], rs[:, 3, :], rs[:, 0, :], ALU.mult))
                link(nc.vector.tensor_scalar(rs[:, 3, :], rs[:, 3, :], -0.5, 1.5, ALU.mult, ALU.add))
                link(nc.vector.tensor_tensor(rs[:, 2, :], rs[:, 2, :], rs[:, 3, :], ALU.mult))

            def normalise(k, dst):
                for t in range(TILES):
                    last = nc.vector.tensor_scalar(dst[:, t, :], xs[:, t, :], mv[:, t, 0:1], rs[:, 2, t:t + 1],
                                                   ALU.subtract, ALU.mult)
                    if t % CT == CT - 1:
                        last.then_inc(xn_done, 1)

            def modulate(k):
                for c in range(CH):
                    v.wait_ge(tr_done, CH * k + c + 1)
                    b = c // 2
                    nc.vector.tensor_scalar(hTf[:, 512 * c:512 * c + 512], ps[:, 4 + c % 2, :],
                                            modT[:, 2 * k + 1, b:b + 1], modT[:, 2 * k, b:b + 1],
                                            ALU.mult, ALU.add).then_inc(hTf_done, 1)

            def hidden_lo(k):
                with v.Fori(0, CH) as c:
                    v.wait_ge(hh_done, CH * k + c + 1)
                    nc.vector.tensor_tensor(hl[:, bass.ds(c * 512, 512)], hTf[:, bass.ds(c * 512, 512)],
                                            hh[:, bass.ds(c * 512, 512)], ALU.subtract).then_inc(hl_done, 1)

            v.wait_ge(mod_ps, 1)
            nc.vector.tensor_copy(modT[:].rearrange("p m b -> p (m b)"), ps[:, 6, 0:8])
            link(nc.vector.tensor_copy(gate[:].rearrange("p m d -> p (m d)"), ps[:, 7, :]))
            for m in (1, 3):
                last = nc.vector.tensor_scalar(modT[:, m, :], modT[:, m, :], 1.0, None, ALU.add)
            link(last)
            link(nc.vector.tensor_scalar(gtmp, gate[:], 0.0, 2.0, ALU.is_ge, ALU.mult))
            link(nc.vector.scalar_tensor_tensor(out=gate[:], in0=gtmp, scalar=-1.0, in1=gate[:],
                                                op0=ALU.add, op1=ALU.mult))
            link(nc.vector.tensor_scalar(gate[:], gate[:], 0.25, None, ALU.max))
            link(nc.vector.scalar_tensor_tensor(out=gate[:], in0=gtmp, scalar=-1.0, in1=gate[:],
                                                op0=ALU.add, op1=ALU.mult))
            statistics(0)
            normalise(0, xn)
            modulate(0)
            v.wait_ge(wa_hi, 1)
            nc.vector.tensor_tensor(wal[:], wst, wah[:], ALU.subtract).then_inc(wa_lo, 1)
            hidden_lo(0)
            for b in range(B):
                v.wait_ge(hTf_done, 2 * b + 2)
                if b > 0:
                    v.wait_ge(clo_done, b)
                nc.vector.tensor_tensor_scan(cums, hTf[:, N * b:N * b + N], hTf[:, N * b:N * b + N], 0.0,
                                             ALU.add, ALU.bypass).then_inc(scan_done, 1)
                v.wait_ge(chi_done, b + 1)
                nc.vector.scalar_tensor_tensor(out=cl[:, N * b:N * b + N], in0=cums, scalar=0.5,
                                               in1=ch[:, N * b:N * b + N], op0=ALU.mult, op1=ALU.subtract).then_inc(clo_done, 1)
            for b in range(B):
                v.wait_ge(enc_hi, 4 * b + 2)
                for s in range(2):
                    last = nc.vector.tensor_tensor(kenc_sb[:, b, 1, s, :, 64 * s:64 * s + 64],
                                                   ps[:, 4, 0:128].rearrange("p (g t) -> p g t", g=2),
                                                   kenc_sb[:, b, 0, s, :, 64 * s:64 * s + 64], ALU.subtract)
                last.then_inc(enc_lo, 1)
                v.wait_ge(enc_hi, 4 * b + 4)
                for s in range(2):
                    last = nc.vector.tensor_tensor(vencst[64 * s:64 * s + 64, b, :, HD + 1:2 * HD + 1],
                                                   ps[64 * s:64 * s + 64, 5, :].rearrange("p (a e) -> p a e", e=HD),
                                                   vencst[64 * s:64 * s + 64, b, :, 0:HD], ALU.subtract)
                last.then_inc(enc_lo, 1)

            v.wait_ge(ld_k, 16 * 5)
            for n in range(NP):
                last = nc.vector.tensor_copy(C[:, n, :, :, HD], hc[:, :, None].to_broadcast([P, BT, 2]))
            last.then_inc(count_done, 1)
            v.wait_ge(setup_done, 1)
            with v.Fori(0, CH) as c:
                for u in range(12):
                    bank = ps[:, u % 4, :]
                    if u < 4:
                        v.wait_ge(prj_hi, c * 12 + (u + 1))
                        hi = part_at(("qh", "kh")[u // 2], c, u % 2)
                        lo = part_at(("ql", "kl")[u // 2], c, u % 2)
                        nc.vector.tensor_tensor(lo, bank, hi, ALU.subtract).then_inc(prj_out, 1)
                    elif u < 12:
                        i, half = (u - 4) // 2, u % 2
                        v.wait_ge(prj_hi, c * 12 + (u + 1))
                        pair = vst[:, i % 2, 4 * half:4 * half + 4].rearrange("p a (s v) -> p a s v", s=2)
                        nc.vector.tensor_tensor(pair[:, :, :, HD + 1:2 * HD + 1], bank.rearrange("p (a s e) -> p a s e", a=4, s=2),
                                                pair[:, :, :, 0:HD], ALU.subtract).then_inc(prj_out, 1)
            def low(it, k):
                if k % NU in MASKED or k % NU == 0:
                    n = sum(1 for j in range(k + 1) if j % NU in MASKED or j % NU == 0)
                    v.wait_ge(mk_done, it * (2 * (len(MASKED) + 1)) + n)
                else:
                    v.wait_ge(sq_done, it * (2 * NU) + (k + 1))
                a = A32[k % A_BUFS]
                hi = a.bitcast(BF16).rearrange("p (n two) -> p n two", two=2)[:, :, 1]
                nc.vector.tensor_tensor(Alo[k % A_BUFS], a, hi, ALU.subtract).then_inc(lo_done, 1)

            def evacuate(it, k):
                hf = k // NU
                v.wait_ge(av_done, it * (2 * NU) + (k + 1 + A_BUFS))
                for s, half in DONE_AFTER[k % NU]:
                    acc_c = C[:, bass.ds(it * 2 + hf, 1), 4 * half:4 * half + 4, s, :].rearrange("p a t e -> p (a t) e")
                    y = ps[:, 4 + 2 * s + half, 0:4 * (HD + 1)].rearrange("p (t e) -> p t e", t=4)
                    nc.vector.tensor_tensor(acc_c, y, acc_c, ALU.add).then_inc(y_free, 1)

            v.sem_inc(y_free, 4)
            with v.Fori(0, NP // 2) as it:
                for k in range(2 * NU):
                    low(it, k)
                    if k >= 2 and (k - 2) % NU in DONE_AFTER:
                        evacuate(it, k - 2)
                evacuate(it, 2 * NU - 1)

            v.sem_inc(at_lo, 2)
            v.sem_inc(g_done, 2)
            v.wait_ge(y_free, 4 * NP + 4)
            nc.vector.tensor_scalar(zr[:], C[:, :, :, :, HD], EPS, None, ALU.add).then_inc(z0, 1)
            v.wait_ge(z0, 1)
            nc.vector.reciprocal(zr[:], zr[:]).then_inc(z_done, 1)
            with v.Fori(0, BT) as t:
                for b in range(B):
                    v.wait_ge(at_hi, t * 2 + (b + 1))
                    nc.vector.tensor_tensor(aTl[b].rearrange("p a t -> p (a t)"), Sb[b], aTh[b].rearrange("p a t -> p (a t)"),
                                            ALU.subtract).then_inc(at_lo, 1)
                for b in range(B):
                    xt = xs[:, bass.ds(t + BT * b, 1), :].rearrange("p a d -> p (a d)")
                    v.wait_ge(o_ps, t * 2 + (b + 1) + 2)
                    nc.vector.tensor_tensor(tmp[b], ps[:, 4 + b, 0:D], gate[:, b, :], ALU.mult).then_inc(g_done, 1)
                    v.wait_ge(g_done, t * 2 + (b + 1) + 2)
                    nc.vector.tensor_tensor(xt, xt, tmp[b], ALU.add).then_inc(x1_done, 1)
                    v.wait_ge(x1_done, t * 2 + (b + 1))
                    nc.vector.bn_stats(stats[:, bass.ds(t + BT * b, 1), :].rearrange("p a d -> p (a d)"), xt).then_inc(st_done, 1)
            statistics(1)
            normalise(1, xn2)
            modulate(1)
            hidden_lo(1)
            v.wait_ge(ld_b2, 16 * 5)
            v.wait_ge(sc_ps, 1)
            sc = sco
            link(nc.vector.tensor_tensor(sc, ps[:, 6, 0:TILES * E].rearrange("p (t e) -> p t e", e=E),
                                         brs[:, None, :].to_broadcast([P, TILES, E]), ALU.add))
            gt = cmp2[:, 0:TILES]
            eq = cmp2[:, TILES:2 * TILES]
            other = sc[:, :, None, :].to_broadcast([P, TILES, E, E])
            own = sc[:, :, :, None].to_broadcast([P, TILES, E, E])
            nc.vector.tensor_tensor(gt, other, own, ALU.is_gt)
            link(nc.vector.tensor_tensor(eq, other, own, ALU.is_equal))
            for t in range(TILES):
                last = nc.vector.tensor_tensor(eq[:, t], eq[:, t], bef, ALU.mult)
            link(last)
            link(nc.vector.tensor_tensor(gt, gt, eq, ALU.add))
            nc.vector.tensor_reduce(out=rk, in_=gt, axis=AX.X, op=ALU.add)
            link(nc.vector.tensor_reduce(out=mx[:], in_=sc, axis=AX.X, op=ALU.max))
            mask = cmp2[:, 0:2].rearrange("p a b c -> p (a b c)").rearrange("p (t e) -> p t e", e=E)
            link(nc.vector.tensor_scalar(mask, rk, 2.0, None, ALU.is_lt))
            nc.vector.tensor_tensor(rk, sc, mx[:, :, None].to_broadcast([P, TILES, E]), ALU.subtract).then_inc(rt, 1)
            v.wait_ge(exp_done, 1)
            link(nc.vector.tensor_tensor(rk, rk, mask, ALU.mult))
            link(nc.vector.tensor_reduce(out=mx[:], in_=rk, axis=AX.X, op=ALU.add))
            nc.vector.memset(wts, 0.0)
            link(nc.vector.reciprocal(mx[:], mx[:]))
            nc.vector.tensor_tensor(wts[:, :, 0:E], rk, mx[:, :, None].to_broadcast([P, TILES, E]), ALU.mult).then_inc(w_ready, 1)
            v.wait_ge(wt_ps, 1)
            nc.vector.tensor_copy(wT.rearrange("p a t -> p (a t)"), ps[:, 6, :]).then_inc(wt_done, 1)
            v.wait_ge(b2_ps, 1)
            nc.vector.tensor_copy(acc.rearrange("p (q i) d -> p i q d", i=4),
                                  ps[:, 0:4, :].rearrange("p i (q d) -> p i q d", d=D)).then_inc(acc_done, 1)
            v.wait_ge(acc_done, 1)
            v.sem_inc(dn_free, 2)
            with v.Fori(0, CH) as c:
                def accumulate(e):
                    v.wait_ge(dn_ps, c * E + (e + 1) + 2)
                    v.wait_ge(dn_free, c * E + (e + 2))
                    for i in range(CT):
                        at = acc[:, bass.ds(c * CT + i, 1), :].rearrange("p a d -> p (a d)")
                        last = nc.vector.scalar_tensor_tensor(
                            out=at, in0=ps[:, 4 + e % 2, i * D:(i + 1) * D],
                            scalar=wts[:, bass.ds(c * CT + i, 1), e:e + 1].rearrange("p a b -> p (a b)"),
                            in1=at, op0=ALU.mult, op1=ALU.add)
                    last.then_inc(dn_free, 1)

                for e in range(E):
                    for j in range(2):
                        v.wait_ge(g_ok, c * (E * PT) + (e * PT + 2 * j + 2 + PT))
                        g = G[e % 2][:, 2 * j:2 * j + 2, :]
                        hi = g.bitcast(BF16).rearrange("p a (n two) -> p a n two", two=2)[:, :, :, 1]
                        nc.vector.tensor_tensor(Glo[e % 2][:, 2 * j:2 * j + 2, :], g, hi, ALU.subtract).then_inc(glo, 1)
                    if e:
                        accumulate(e - 1)
                accumulate(E - 1)
                v.wait_ge(dn_free, c * E + (E + 2))
                at = acc[:, bass.ds(c * CT, CT), :]
                row = gate[:, bass.ds(c // 2 + 2, 1), :].to_broadcast([P, CT, D])
                nc.vector.tensor_tensor(at, at, row, ALU.mult).then_inc(fstep, 1)
                v.wait_ge(fstep, c + 1)
                nc.vector.tensor_tensor(at, at, xs[:, bass.ds(c * CT, CT), :], ALU.add).then_inc(fin_done, 1)

        @block.tensor
        def _(pe):
            mm = nc.tensor.matmul

            def three(dst, sh, sl, mh, ml):
                mm(dst, sh, mh, start=True, stop=False)
                mm(dst, sh, ml, start=False, stop=False)
                return mm(dst, sl, mh, start=False, stop=True)

            def transposes(k, src):
                for c in range(CH):
                    pe.wait_ge(xn_done, CH * k + c + 1)
                    if c >= 2:
                        pe.wait_ge(hTf_done, CH * k + c - 1)
                    for i in range(CT):
                        last = nc.tensor.transpose(ps[:, 4 + c % 2, i * P:(i + 1) * P], src[:, CT * c + i, :], id32[:])
                    last.then_inc(tr_done, 1)

            pe.wait_ge(ld_c, 32)
            pe.wait_ge(silu_done, 1)
            for m, col in enumerate((0, 1, 3, 4)):
                mm(ps[:, 6, 2 * m:2 * m + 2], wms[:, col * D:(col + 1) * D], scT[:], start=True, stop=True)
            pe.wait_ge(scb_done, 1)
            for m, col in enumerate((2, 5)):
                for b in range(B):
                    last = mm(ps[:, 7, (2 * m + b) * D:(2 * m + b + 1) * D], scb[:, b, :], wms[:, col * D:(col + 1) * D],
                              start=True, stop=True)
            last.then_inc(mod_ps, 1)
            pe.wait_ge(ld_k, 16 * 5)
            transposes(0, xn)

            pe.wait_ge(wa_lo, 1)
            pe.wait_ge(hl_done, CH)
            pe.wait_ge(clo_done, B)
            for b in range(B):
                if b:
                    pe.wait_ge(enc_lo, 2 * b - 1)
                t = slice(N * b, N * b + ENC)
                for g in range(2):
                    w = slice(KE0 + P * g, KE0 + P * (g + 1))
                    last = three(ps[:, 4, ENC * g:ENC * (g + 1)], wah[:, w], wal[:, w], hh[:, t], hl[:, t])
                last.then_inc(enc_ps, 1)
                if b:
                    pe.wait_ge(enc_lo, 2 * b)
                for s in range(2):
                    w = slice(VE0 + 512 * s, VE0 + 512 * (s + 1))
                    last = three(ps[64 * s:64 * s + 64, 5, :], hh[:, t], hl[:, t], wah[:, w], wal[:, w])
                last.then_inc(enc_ps, 1)
            with pe.Fori(0, CH) as c:
                for u in range(TOTAL_PRJ):
                    if u < 4:
                        pe.wait_ge(prj_c, c * 8 + (u + 5))
                    elif u < 16:
                        pe.wait_ge(prj_out, c * 12 + (u - 3))
                    else:
                        pe.wait_ge(prj_c, c * 8 + (u - 15 + 8))
                    bank = ps[:, u % 4, :]
                    if u < 4:
                        w = Q0 + P * u
                        last = three(bank, wah[:, w:w + P], wal[:, w:w + P],
                                     hh[:, bass.ds(c * 512, 512)], hl[:, bass.ds(c * 512, 512)])
                    else:
                        i, w = ((u - 4) % 8) // 2, V0 + 512 * (u % 2)
                        xh, xl = (hh, hl) if u < 12 else (ch, cl)
                        last = three(bank, xh[:, bass.ds(c * 512 + P * i, P)], xl[:, bass.ds(c * 512 + P * i, P)],
                                     wah[:, w:w + 512], wal[:, w:w + 512])
                    last.then_inc(prj_ps, 1)
            def scores(it, k):
                hf, unit = (k // NU) % 2, UNITS[k % NU]
                if k % NU == 0:
                    pe.wait_ge(slot[hf], it * 112 + 112 * (1 + k // (2 * NU)))
                if k >= S_BUFS:
                    pe.wait_ge(sq_done, it * (2 * NU) + (k + 1 - S_BUFS))
                for off, w, s, j, q0 in unit:
                    col = 2 * N if j == "enc" else N * s + P * j
                    last = mm(Sb[k % S_BUFS][:, off:off + w], kS[hf][:, col:col + P], qS[hf][:, q0:q0 + w], start=True, stop=True)
                last.then_inc(s_ready, 1)

            def products(hf, k, blocks, first):
                a = A32[k % A_BUFS]
                hi = a.bitcast(BF16).rearrange("p (n two) -> p n two", two=2)[:, :, 1]
                for n, (off, s, j, i) in enumerate(blocks):
                    y = ps[:, 4 + 2 * s + i // 4, (i % 4) * (HD + 1):(i % 4 + 1) * (HD + 1)]
                    t = VW * (2 * (BT if j == "enc" else j) + s)
                    vv = vS[hf][:, t:t + VW]
                    one = dict(start=False, stop=True, skip_group_check=True)
                    mm(y, hi[:, off:off + P], vv[:, 0:HD + 1], start=first and n == 0, stop=True, skip_group_check=True)
                    mm(y[:, 0:HD], hi[:, off:off + P], vv[:, HD + 1:2 * HD + 1], **one)
                    last = mm(y, Alo[k % A_BUFS][:, off:off + P], vv[:, 0:HD + 1], **one)
                return last

            def weighted(it, k):
                hf, kk = k // NU, k % NU
                pe.wait_ge(lo_done, it * (2 * NU) + (k + 1))
                if kk == 0:
                    for n, (s, half) in enumerate(GROUPS[:3]):
                        pe.wait_ge(y_free, it * 8 + (4 * hf + n + 1))
                        products(hf, k, [(512 * half + P * m, s, "enc", 4 * half + m) for m in range(4)], True)
                    return
                blocks = [(off + P * m, s, j, q0 // P + m) for off, w, s, j, q0 in UNITS[kk] for m in range(w // P)]
                last = products(hf, k, blocks, False)
                if kk == 1:
                    s, half = GROUPS[3]
                    pe.wait_ge(y_free, it * 8 + (4 * hf + 4))
                    last = products(hf, k - 1, [(512 * half + P * m, s, "enc", 4 * half + m) for m in range(4)], True)
                last.then_inc(av_done, 2 if kk == 1 else 1)

            pe.wait_ge(prj_c, 8 * CH + 8)
            pe.sem_inc(av_done, A_BUFS)
            for k in range(LAG):
                scores(0, k)
            with pe.Fori(0, NP // 2 - 1) as it:
                for k in range(2 * NU):
                    scores(it, k + LAG)
                    weighted(it, k)
            for k in range(2 * NU):
                if k + LAG < 2 * NU:
                    scores(NP // 2 - 1, k + LAG)
                weighted(NP // 2 - 1, k)

            pe.sem_inc(at_ps, 2)
            pe.sem_inc(o_ps, 2)
            with pe.Fori(0, BT) as t:
                for b in range(B):
                    pe.wait_ge(an_done, t * 2 + (b + 1))
                    pe.wait_ge(at_lo, t * 2 + (b + 1))
                    for p in range(PAIRS):
                        last = nc.tensor.transpose(Sb[b][:, P * p:P * (p + 1)],
                                                   an[b][:, 2 * p:2 * p + 2, :].rearrange("p s e -> p (s e)"), id32[:])
                    last.then_inc(at_ps, 1)
                for b in range(B):
                    pe.wait_ge(at_lo, t * 2 + (b + 1) + 2)
                    pe.wait_ge(g_done, t * 2 + (b + 1))
                    bank = ps[:, 4 + b, 0:D]
                    for p in range(PAIRS):
                        w = slice(O0 + D * p, O0 + D * (p + 1))
                        mm(bank, aTh[b][:, p, :], wah[:, w], start=p == 0, stop=False)
                        mm(bank, aTh[b][:, p, :], wal[:, w], start=False, stop=False)
                        last = mm(bank, aTl[b][:, p, :], wah[:, w], start=False, stop=p == PAIRS - 1)
                    last.then_inc(o_ps, 1)

            transposes(1, xn2)
            pe.wait_ge(hTf_done, 2 * CH)
            for t in range(TILES):
                last = mm(ps[:, 6, E * t:E * (t + 1)], hTf[:, P * t:P * (t + 1)], wrs[:], start=True, stop=True)
            last.then_inc(sc_ps, 1)
            pe.wait_ge(w_ready, 1)
            for q in range(4):
                last = nc.tensor.transpose(ps[:, 6, P * q:P * (q + 1)], wts[:, 4 * q:4 * q + 4, :].rearrange("p t e -> p (t e)"), id32[:])
            last.then_inc(wt_ps, 1)
            pe.wait_ge(wt_done, 1)
            for t in range(TILES):
                r = slice(32 * (t % 4), 32 * (t % 4) + E)
                last = mm(ps[:, t % 4, D * (t // 4):D * (t // 4 + 1)], wT[r, t // 4, :], b2s[r, :], start=True, stop=True)
            last.then_inc(b2_ps, 1)

            pe.wait_ge(hl_done, 2 * CH)
            pe.wait_ge(ff_split, 4)
            pe.sem_inc(dn_ps, 2)

            with pe.Fori(0, CH) as c:
                def up(e):
                    for pt in range(PT):
                        pe.wait_ge(g_ok, c * (E * PT) + (e * PT + pt + 1))
                        w = slice(P * pt, P * (pt + 1))
                        three(ps[:, pt, :], w1h[:, e, w], w1l[:, e, w], hh[:, bass.ds(c * 512, 512)],
                              hl[:, bass.ds(c * 512, 512)]).then_inc(up_ps, 1)

                def down(e):
                    pe.wait_ge(dn_free, c * E + (e + 1))
                    pe.wait_ge(glo, c * (2 * E) + (2 * e + 2))
                    hi = G[e % 2].bitcast(BF16).rearrange("p a (n two) -> p a n two", two=2)[:, :, :, 1]
                    for i in range(CT):
                        bank, t = ps[:, 4 + e % 2, i * D:(i + 1) * D], slice(P * i, P * (i + 1))
                        for pt in range(PT):
                            mm(bank, hi[:, pt, t], w2h[:, e, pt, :], start=pt == 0, stop=False)
                            mm(bank, hi[:, pt, t], w2l[:, e, pt, :], start=False, stop=False)
                            last = mm(bank, Glo[e % 2][:, pt, t], w2h[:, e, pt, :], start=False, stop=pt == PT - 1)
                    last.then_inc(dn_ps, 1)

                up(0)
                for e in range(1, E):
                    up(e)
                    down(e - 1)
                down(E - 1)


def kernel(L0_attn_x, L0_attn_Wq, L0_attn_Wk, L0_attn_Wv, L0_attn_Wk_enc, L0_attn_Wv_enc, L0_attn_Wout,
           L0_ffn_W1, L0_ffn_b1, L0_ffn_W2, L0_ffn_b2, L0_ffn_Wr, L0_ffn_br, L0_c, L0_wmod):
    import numpy as np
    import concourse.bacc as bacc
    from concourse.bass_utils import run_bass_kernel_spmd

    a = np.asarray

    def groups(w):
        return a(w).reshape(4, 2, 2, FD, D).transpose(4, 1, 2, 0, 3).reshape(D, 256)

    wo = a(L0_attn_Wout).T.reshape(PAIRS, P, D).transpose(1, 0, 2).reshape(P, PAIRS * D)
    ve = a(L0_attn_Wv_enc).reshape(PAIRS, 2, HD, D).transpose(3, 1, 0, 2).reshape(D, H * HD)
    arrays = {
        "x": a(L0_attn_x).reshape(TILES, P, D),
        "wqkT": np.concatenate([groups(L0_attn_Wq), groups(L0_attn_Wk), groups(L0_attn_Wk_enc)], axis=1),
        "wvT": np.concatenate([a(L0_attn_Wv).T, ve], axis=1),
        "woT": wo,
        "w1": a(L0_ffn_W1).transpose(1, 0, 2).reshape(D, E * PF),
        "b1T": a(L0_ffn_b1).reshape(E, PT, P).transpose(2, 0, 1),
        "w2": a(L0_ffn_W2).reshape(E, PT, P, D).transpose(2, 0, 1, 3).reshape(P, E * PT * D),
        "b2": a(L0_ffn_b2),
        "wr": a(L0_ffn_Wr),
        "br": a(L0_ffn_br),
        "cT": a(L0_c).T,
        "wmod": a(L0_wmod),
        "ident": np.eye(P, dtype=np.float32),
        "half_count": (0.5 * (P * np.arange(BT)[None, :] + np.arange(P)[:, None] + 1)).astype(np.float32),
        "before": np.broadcast_to(np.tril(np.ones((E, E), np.float32), -1), (P, E, E)),
    }
    nc = bacc.Bacc("TRN2", target_bir_lowering=False, num_devices=1)
    args = {}
    feed = {}
    for name, value in arrays.items():
        feed[name + "_dram"] = np.ascontiguousarray(value)
        args[name] = nc.dram_tensor(name + "_dram", value.shape, F32, kind="ExternalInput").ap()
    out = nc.dram_tensor("out_dram", (TILES, P, D), F32, kind="ExternalOutput").ap()
    adaln_block(nc, out=out, **args)
    r = run_bass_kernel_spmd(nc, [feed], core_ids=[0])
    return r.results[0]["out_dram"].reshape(B, N, D)
```

```python
from contextlib import ExitStack

import concourse.bass as bass
from concourse import mybir

F32 = mybir.dt.float32
F16 = mybir.dt.float16
BF16 = mybir.dt.bfloat16
ACT = mybir.ActivationFunctionType
ALU = mybir.AluOpType
AX = mybir.AxisListType

P = 128
B, N, D = 2, 1024, 128
H, FD, HD = 16, 16, 64
ENC = 64
E, PF = 8, 512
PT = PF // P
TILES = B * N // P
BT = N // P
PAIRS = H // 2
NP = B * PAIRS
CH = 4
CT = TILES // CH
VW = 130
VROW = 2 * (BT + 1) * VW
EPS = 1e-12
LN_EPS = 1e-5
SQ_SCALE = 0.25 * 2.0 ** -0.5
SQ_BIAS = 2.0 ** -0.5
A_BUFS = 5
S_BUFS = 2
LAG = 4
PI = 4

def _units():
    first = lambda s: [(0, 512, s, 0, 0), (512, 384, s, 1, 128), (896, 128, s, 3, 384)]
    full = lambda s, j: [(0, 512, s, j, 512), (512, 512, s, j + 1, 512)]
    last = lambda s: [(0, 512, s, 4, 512), (512, 384, s, 5, 640), (896, 128, s, 7, 896)]
    mid = [(0, 256, 0, 2, 256), (256, 256, 0, 6, 768), (512, 256, 1, 2, 256), (768, 256, 1, 6, 768)]
    enc = [(0, 512, None, "enc", 0), (512, 512, None, "enc", 512)]
    return [enc, first(0), first(1), mid, full(0, 0), full(0, 2), last(0), full(1, 0), full(1, 2), last(1)]


UNITS = _units()
NU = len(UNITS)
IU = PI * NU
MASKED = (1, 2, 3, 6, 9)
POOL_LOW = (4, 7)
DONE_AFTER = {3: [(0, 0), (1, 0)], 6: [(0, 1)], 9: [(1, 1)]}
GROUPS = [(0, 0), (1, 0), (0, 1), (1, 1)]


def adaln_block(nc, x, wqkT, wvT, woT, w1, b1T, w2, b2, wr, br, cT, wmod, ident, half_count, index_order, out):
    ctx = ExitStack()
    with ctx:
        def sb(name, shape, dt):
            return ctx.enter_context(nc.sbuf_tensor(name, shape, dt))

        def sem(name):
            return ctx.enter_context(nc.semaphore(name))

        xs = sb("xs", [P, TILES, D], F32)
        hTf = sb("hTf", [P, TILES * P], F32)
        hh = sb("hh", [P, TILES * P], F16)
        hl = sb("hl", [P, TILES * P], F16)
        ch = sb("ch", [P, TILES * P], F16)
        cl = sb("cl", [P, TILES * P], F16)
        WA = 3 * 256 + 3 * 1024
        wah = sb("wah", [P, WA], F16)
        wal = sb("wal", [P, WA], F16)
        Q0, K0, KE0, V0, VE0, O0 = 0, 256, 512, 768, 768 + 1024, 768 + 2048
        w1h = sb("w1h", [P, E, PF], F16)
        w1l = sb("w1l", [P, E, PF], F16)
        w2h = sb("w2h", [P, E, PT, D], F16)
        w2l = sb("w2l", [P, E, PT, D], F16)
        C = sb("C", [P, NP, BT, 2, HD + 1], F32)
        vst = sb("vst", [P, 2, PAIRS, 2 * VW], F16)
        id32 = sb("id32", [P, P], F32)
        arena = sb("arena", [P, 49152 // 4], F32)

        def view(byte, shape, dt):
            n = 1
            for s in shape:
                n *= s
            size = n * (4 if dt == F32 else 2)
            a = arena[:, byte // 4:(byte + size) // 4]
            if dt != F32:
                a = a.bitcast(dt)
            if len(shape) > 1:
                names = "abcd"[:len(shape)]
                a = a.rearrange(f"p ({' '.join(names)}) -> p {' '.join(names)}",
                                **{n_: s for n_, s in zip(names, shape)})
            return a

        xn = view(0, [TILES, D], F32)
        wst = view(8192, [WA], F32)
        wms = view(8192 + WA * 4, [6 * D], F32)
        cums = [view(4 * N * b, [N], F32) for b in range(B)]
        ffs = view(32768, [E * PF], F32)
        plain = {n_: view(8192 * i, [B, 2, N], F16) for i, n_ in enumerate(("qh", "ql", "kh", "kl"))}
        A32 = [view(4096 * i, [1024], F32) for i in range(4)] + [ch[:].bitcast(F32)]
        Alo = [view(16384 + 2048 * i, [1024], F16) for i in range(4)] + [cl[:, 0:1024]]
        SLOT = 2 * (N + 2 * N + P + VROW)
        SLOT0 = 49152 - 1024 - 2 * SLOT
        qS = [view(SLOT0 + SLOT * i, [N], F16) for i in range(2)]
        kS = [view(SLOT0 + SLOT * i + 2 * N, [2 * N + P], F16) for i in range(2)]
        vS = [view(SLOT0 + SLOT * i + 2 * (3 * N + P), [VROW], F16) for i in range(2)]
        an = [view(4096 * i, [H, HD], F32) for i in range(2)]
        aTh = [view(8192 + 2048 * i, [PAIRS, P], F16) for i in range(2)]
        aTl = [view(12288 + 2048 * i, [PAIRS, P], F16) for i in range(2)]
        tmp = [view(16384 + 512 * i, [D], F32) for i in range(2)]
        xn2 = view(24576, [TILES, D], F32)
        G = [view(8192 * i, [PT, 512], F32) for i in range(2)]
        Glo = [view(16384 + 4096 * i, [PT, 512], F16) for i in range(2)]
        acc = view(32768, [TILES, D], F32)

        kenc_sb = hTf[:, 0:N].bitcast(F16).rearrange("p (b c s g t) -> p b c s g t", b=B, c=2, s=2, g=2)
        kenc = [[[kenc_sb[:, b, part, s] for s in range(2)] for part in range(2)] for b in range(B)]
        vencst = sb("vencst", [P, B, PAIRS, VW], F16)
        stats = view(31744, [TILES, 6], F32)
        mv = sb("mv", [P, TILES, 2], F32)
        rs = sb("rs", [P, 4, TILES], F32)
        cs = sb("cs", [P, B], F32)
        scT = sb("scT", [P, B], F32)
        scb = view(30720, [B, P], F32)
        modT = sb("modT", [P, 4, B], F32)
        gate = sb("gate", [P, 4, P], F32)
        gtmp = view(8192 + WA * 4 + 6 * D * 4, [4, P], F32)
        hc = sb("hc", [P, BT], F32)
        sqb = sb("sqb", [P, 1], F32)
        zr = view(18432, [NP, BT, 2], F32)
        wrs = sb("wrs", [P, E], F32)
        brs = sb("brs", [P, E], F32)
        b1s = sb("b1s", [P, E, PT], F32)
        b2s = view(45056, [4, D], F32)
        sco = view(24576, [TILES, E], F32)
        rk = view(25088, [TILES, E], F32)
        cand = view(25600, [TILES, E], F32)
        best = view(26112, [TILES, E], F32)
        second = view(26624, [TILES, E], F32)
        top = view(27136, [2, TILES], F32)
        order = sb("order", [P, E], F32)
        mx = sb("mx", [P, TILES], F32)
        wts = view(40960, [TILES, 32], F32)
        wT = view(43008, [P], F32)
        wc = view(43520, [4, 32], F32)

        ps = ctx.enter_context(nc.psum_tensor("ps", [P, 8, 512], F32))
        Sb = [ps[:, 2 * i:2 * i + 2, :].rearrange("p a b -> p (a b)") for i in range(2)]

        sQ = nc.dram_tensor("scratch_q", [B, P, PAIRS, N], F16, kind="Internal").ap()
        sK = nc.dram_tensor("scratch_k", [B, P, PAIRS, N], F16, kind="Internal").ap()
        sKE = nc.dram_tensor("scratch_k_enc", [B, P, PAIRS, P], F16, kind="Internal").ap()
        sV = nc.dram_tensor("scratch_v", [NP, P, VROW], F16, kind="Internal").ap()

        ld_c = sem("c_loaded"); ld_wm = sem("wmod_loaded"); ld_id = sem("identity_loaded"); ld_hc = sem("half_counts_loaded"); ld_x = [sem(f"x_loaded{q}") for q in range(CH)]; ld_wa = sem("attn_weights_loaded")
        ld_w1 = sem("w1_loaded"); ld_w2 = sem("w2_loaded"); ld_k = sem("consts_loaded"); ld_b2 = sem("b2_loaded")
        silu_done = sem("silu_done"); scb_done = sem("silu_broadcast")
        mod_ps = sem("mod_products"); mod_out = sem("modulation_banks_read")
        gate_step = sem("gate_step"); gate_done = sem("gate_done")
        wa_hi = sem("wa_hi"); wa_lo = sem("wa_lo"); ff_split = sem("ffn_split")
        setup_done = sem("setup_done"); kenc_zero = sem("kenc_zeroed"); pool_turn = sem("pool_turn"); enc_stored = sem("encoder_stored"); slot_zeroed = sem("slots_zeroed")
        st_done = sem("bn_stats_done"); agg_done = sem("bn_aggr_done")
        var_done = sem("var_plus_eps"); std_done = sem("std_done"); rstd_step = sem("rstd_step")
        xn_done = sem("xn_done"); tr_done = sem("transposed"); hTf_done = sem("hTf_done")
        hh_done = sem("hh_done"); hl_done = sem("hl_done")
        scan_done = sem("scan_done"); chi_done = sem("cum_hi"); clo_done = sem("cum_lo")
        prj_ps = sem("projection_products"); prj_hi = sem("projection_hi"); prj_out = sem("projection_out"); v_ps = sem("v_products"); c_ps = sem("running_sum_products"); v_hi = sem("v_hi"); v_out = sem("v_out")
        prj_free = sem("projection_bank_free")
        v_stored = [sem("v_stored_even"), sem("v_stored_odd")]; stacked = [sem("stacked_batch0"), sem("stacked_batch1")]
        enc_ps = sem("enc_products"); enc_hi = sem("enc_hi"); enc_lo = sem("enc_lo")
        slot = [sem("slot0_loaded"), sem("slot1_loaded")]
        s_ready = sem("scores_ready");
        sq_done = sem("squared"); mk_done = sem("masked"); lo_done = sem("a_lo_done"); lo_pool = sem("a_lo_done_by_pool")
        av_done = sem("a_buffers_free_and_units_done")
        y_free = sem("y_bank_free")
        z_done = sem("z_done"); an_done = sem("normalized"); at_ps = sem("attn_transposed")
        at_hi = sem("attnT_hi"); at_lo = sem("attnT_lo"); o_ps = sem("out_products"); g_done = sem("gated")
        x1_done = sem("x1_done")
        sc_ps = sem("router_products"); rt = sem("router_step"); exp_done = sem("exp_done")
        w_ready = sem("expert_weights_ready"); wts_zeroed = sem("wts_zeroed"); wc_done = sem("chunk_weights_copied"); wt_ps = sem("weights_transposed"); wt_done = sem("wT_done")
        up_ps = sem("up_products"); g_ok = sem("gelu_done"); glo = sem("gelu_lo"); up_free = sem("g_buffer_free")
        dn_ps = sem("down_products"); acc_done = sem("accumulated"); b2_ps = sem("b2_products"); b2_zeroed = sem("b2_blocks_zeroed"); b2_read = sem("b2_part_read")
        fin_done = sem("final_done"); out_done = sem("out_stored"); fstep = sem("final_step")

        prj_c = sem("running_sums_out"); count_done = sem("half_counts_in_C"); chain = sem("vector_chain"); z0 = sem("den_ready"); dn_free = sem("down_bank_free")

        def part_at(name, c, g):
            return plain[name][:, bass.ds(c // 2, 1), g, bass.ds((c % 2) * 512, 512)].rearrange("p a t -> p (a t)")

        def sums_at(it, i, half):
            at = C[:, bass.ds((it // (BT // 2)) * PAIRS + 4 * half, 4), bass.ds((it % (BT // 2)) * 2 + i, 1), :, 0:HD]
            return at.rearrange("p n a s e -> p (n a) s e")

        block = ctx.enter_context(nc.Block())

        @block.sync
        def _(sp):
            sp.dma_start(cs[:], cT).then_inc(ld_c, 16)
            sp.dma_start(hc[:], half_count).then_inc(ld_hc, 16)
            for q in range(4):
                sp.dma_start(xs[:, CT * q:CT * q + CT, :],
                             x[CT * q:CT * q + CT].rearrange("t p d -> p t d")).then_inc(ld_x[q], 16)
            sp.dma_start(wms, wmod).then_inc(ld_wm, 16)
            sp.dma_start(id32[:], ident).then_inc(ld_id, 16)
            sp.dma_start(wst[:, 0:V0], wqkT).then_inc(ld_wa, 16)
            sp.dma_start(wst[:, V0:O0], wvT).then_inc(ld_wa, 16)
            sp.dma_start(wst[:, O0:WA], woT).then_inc(ld_wa, 16)
            sp.dma_start(ffs, w1).then_inc(ld_w1, 16)
            for dst, src in ((wrs[:], wr), (b1s[:], b1T), (order[:], index_order)):
                sp.dma_start(dst, src).then_inc(ld_k, 16)
            sp.dma_start(brs[:], br.partition_broadcast(P)).then_inc(ld_k, 16)
            def store_v(t):
                sp.wait_ge(v_out, 2 * (t + 1) + 2)
                b, at = t // BT, 2 * VW * (t % BT)
                sp.dma_start(sV[PAIRS * b:PAIRS * (b + 1), :, at:at + 2 * VW].rearrange("n p v -> p n v"),
                             vst[:, t % 2]).then_inc(v_stored[t % 2], 16)

            def store_encoder_keys(b, s, r):
                to = sKE[b, 64 * s + 16 * r:64 * s + 16 * r + 16].rearrange("i (k g) t -> k i (g t)", g=2)
                sp.dma_start(to, kenc[b][r // 2][s][64 * s:64 * s + 64].rearrange("p g t -> p (g t)")).then_inc(enc_stored, 16)

            def store_encoder_values(b, s):
                rows, col = slice(64 * s, 64 * s + 64), VW * (2 * BT + s)
                sp.dma_start(sV[PAIRS * b:PAIRS * (b + 1), rows, col:col + VW].rearrange("n p v -> p n v"),
                             vencst[rows, b]).then_inc(enc_stored, 16)

            sp.sem_inc(v_stored[0], 16)
            sp.sem_inc(v_stored[1], 16)
            sp.wait_ge(enc_lo, 2 * B)
            for t in range(TILES):
                store_v(t)
                if t == 6:
                    sp.wait_ge(ff_split, 2)
                    sp.dma_start(ffs, w2).then_inc(ld_w2, 16)
                if t < BT:
                    store_encoder_keys(t // 4, t % 2, t // 2 % 2)
                    store_encoder_keys(t // 4, t % 2, t // 2 % 2 + 2)
                elif t < BT + 4:
                    store_encoder_values((t - BT) // 2, t % 2)

            def load(n, hf):
                lo, hi, V2 = slice(0, 64), slice(64, P), 2 * VW * BT
                for dst, src, rows in ((qS[hf], sQ, slice(0, P)), (kS[hf][lo, 0:N], sK, lo), (kS[hf][hi, N:2 * N], sK, hi),
                                       (kS[hf][:, 2 * N:], sKE, slice(0, P))):
                    at = src[bass.ds(n // PAIRS, 1), rows, bass.ds(n % PAIRS, 1), :]
                    sp.dma_start(dst, at.rearrange("a p n t -> (a p) (n t)")).then_inc(slot[hf], 16)
                for rows, c0, c1 in ((slice(0, P), 0, V2), (lo, V2, V2 + VW), (hi, V2 + VW, V2 + 2 * VW)):
                    sp.dma_start(vS[hf][rows, c0:c1], sV[bass.ds(n, 1), rows, c0:c1].rearrange("a p t -> (a p) t"))\
                      .then_inc(slot[hf], 16)

            sp.wait_ge(enc_stored, 16 * B * (8 + 2))
            sp.wait_ge(slot_zeroed, 1)
            sp.wait_ge(stacked[0], 16 * 16)
            for hf in range(2):
                sp.wait_ge(v_stored[hf], 16 * (BT // 2 + 1))
            load(0, 0)
            load(1, 1)
            sp.wait_ge(stacked[1], 16 * 16)
            for hf in range(2):
                sp.wait_ge(v_stored[hf], 16 * (TILES // 2 + 1))
            with sp.Fori(0, NP // 2 - 1) as it:
                for hf in range(2):
                    sp.wait_ge(av_done, it * (2 * NU) + (NU * (hf + 1) + A_BUFS))
                    load(it * 2 + (hf + 2), hf)
            sp.wait_ge(b2_zeroed, 1)
            for i in range(4):
                sp.dma_start(b2s[32 * i:32 * i + E, i, :], b2).then_inc(ld_b2, 16)
            with sp.Fori(0, CH) as c:
                sp.wait_ge(fin_done, c + 1)
                sp.dma_start(out[bass.ds(c * CT, CT)].rearrange("t p d -> p t d"), acc[:, bass.ds(c * CT, CT), :]).then_inc(out_done, 16)
            sp.wait_ge(out_done, 16 * CH)

        @block.gpsimd
        def _(gp):
            for hf in range(2):
                gp.memset(vst[:, hf].rearrange("p a (s v) -> p a s v", s=2)[:, :, :, HD:HD + 1], 1.0)
                gp.memset(vencst[:, hf, :, HD:HD + 1], 1.0)
                gp.memset(vencst[:, hf, :, VW - 1:VW], 0.0)
                gp.memset(vst[:, hf].rearrange("p a (s v) -> p a s v", s=2)[:, :, :, VW - 1:VW], 0.0)
            gp.memset(sqb[:], SQ_BIAS).then_inc(setup_done, 1)
            gp.wait_ge(wa_hi, 1)
            gp.tensor_tensor(wal[:], wst, wah[:], ALU.subtract).then_inc(wa_lo, 1)
            def split(hi, lo, n):
                gp.tensor_scalar(hi, ffs, 1.0, 0.0, ALU.mult, ALU.add).then_inc(ff_split, 1)
                gp.wait_ge(ff_split, 2 * n + 1)
                gp.tensor_tensor(lo, ffs, hi, ALU.subtract).then_inc(ff_split, 1)

            def store_stack(b):
                for name, dst, rows in (("qh", sQ, (0, 2)), ("ql", sQ, (1, 3)), ("kh", sK, (0, 1)), ("kl", sK, (2, 3))):
                    for s in range(2):
                        for r in rows:
                            to = dst[b, 64 * s + 16 * r:64 * s + 16 * r + 16].rearrange("i (k g) t -> k i (g t)", g=2)
                            gp.dma_start(to, plain[name][64 * s:64 * s + 64, b].rearrange("p g t -> p (g t)"))\
                              .then_inc(stacked[b], 16)

            gp.wait_ge(scan_done, B)
            gp.wait_ge(hl_done, CH)
            gp.memset(hTf[:, 0:N], 0.0).then_inc(kenc_zero, 1)
            gp.wait_ge(ld_w1, 16)
            split(w1h[:].rearrange("p e f -> p (e f)"), w1l[:].rearrange("p e f -> p (e f)"), 0)
            for b in range(B):
                gp.wait_ge(prj_out, 8 * (b + 1))
                store_stack(b)
            gp.wait_ge(ld_w2, 16)
            split(w2h[:].rearrange("p e a d -> p (e a d)"), w2l[:].rearrange("p e a d -> p (e a d)"), 1)
            for b in range(B):
                gp.wait_ge(stacked[b], 16 * 16)
            gp.wait_ge(ff_split, 4)
            for hf in range(2):
                gp.memset(kS[hf][64:P, 0:N], 0.0)
                gp.memset(kS[hf][0:64, N:2 * N], 0.0)
                gp.memset(vS[hf][64:P, 2 * VW * BT:2 * VW * BT + VW], 0.0)
                last = gp.memset(vS[hf][0:64, 2 * VW * BT + VW:VROW], 0.0)
            last.then_inc(slot_zeroed, 1)

            def tri(ap, blocks):
                return nc.gpsimd.affine_select(out=ap, in_=ap, compare_op=ALU.is_ge, fill=0.0, base=0,
                                               pattern=[[0, blocks], [1, P]], channel_multiplier=-1)

            def squared(it, k):
                gp.wait_ge(sq_done, it * IU + (k + 1))
                gp.sem_inc(pool_turn, 1)

            with gp.Fori(0, NP // PI) as it:
                for k in range(IU):
                    a = A32[k % A_BUFS]
                    kk = k % NU
                    if kk == 0:
                        squared(it, k)
                        gp.tensor_scalar(a, a, 1.0, 0.5, ALU.mult, ALU.add).then_inc(mk_done, 1)
                    elif kk == 3:
                        squared(it, k)
                        tri(a.rearrange("p (b c) -> p b c", b=4)[:, :, 0:P], 4).then_inc(mk_done, 1)
                    elif kk in POOL_LOW:
                        squared(it, k)
                        hi = a.bitcast(BF16).rearrange("p (n two) -> p n two", two=2)[:, :, 1]
                        gp.tensor_tensor(Alo[k % A_BUFS], a, hi, ALU.subtract).then_inc(lo_pool, 1)
                    elif kk in MASKED:
                        squared(it, k)
                        tri(a.rearrange("p (b c) -> p b c", b=2)[:, :, 0:P], 2)
                        tri(a[:, 896:1024].rearrange("p (b c) -> p b c", b=1), 1).then_inc(mk_done, 1)

            gp.wait_ge(z_done, 1)
            gp.memset(b2s, 0.0).then_inc(b2_zeroed, 1)
            gp.memset(wts, 0.0).then_inc(wts_zeroed, 1)
            with gp.Fori(0, BT) as t:
                for b in range(B):
                    src = C[:, PAIRS * b:PAIRS * (b + 1), bass.ds(t, 1), :, 0:HD].rearrange("p n a s e -> p (n a) s e")
                    zz = zr[:, PAIRS * b:PAIRS * (b + 1), bass.ds(t, 1), :].rearrange("p n a s -> p (n a) s")[:, :, :, None]\
                        .to_broadcast([P, PAIRS, 2, HD])
                    gp.wait_ge(at_ps, t * 2 + (b + 1))
                    gp.sem_inc(pool_turn, 1)
                    gp.tensor_tensor(an[b].rearrange("p (n s) e -> p n s e", s=2), src, zz, ALU.mult).then_inc(an_done, 1)

        @block.scalar
        def _(act):
            act.wait_ge(ld_c, 16)
            nc.scalar.activation(scT[:], cs[:], ACT.Silu).then_inc(silu_done, 1)

            def stddev(k):
                act.wait_ge(var_done, k)
                nc.scalar.activation(rs[:, 1, :], rs[:, 0, :], ACT.Sqrt).then_inc(std_done, 1)

            def hidden_hi(k):
                with act.Fori(0, CH) as c:
                    act.wait_ge(hTf_done, CH * k + c + 1)
                    nc.scalar.activation(hh[:, bass.ds(c * 512, 512)], hTf[:, bass.ds(c * 512, 512)], ACT.Copy).then_inc(hh_done, 1)

            stddev(1)
            act.wait_ge(ld_wa, 48)
            nc.scalar.activation(wah[:], wst, ACT.Copy).then_inc(wa_hi, 1)
            hidden_hi(0)
            for b in range(B):
                act.wait_ge(scan_done, b + 1)
                nc.scalar.activation(ch[:, N * b:N * b + N], cums[b], ACT.Copy, scale=0.5).then_inc(chi_done, 1)

            act.wait_ge(kenc_zero, 1)
            for b in range(B):
                act.wait_ge(enc_ps, 2 * b + 1)
                for s in range(2):
                    nc.scalar.activation(kenc_sb[:, b, 0, s, :, 64 * s:64 * s + 64],
                                         ps[:, 4 + 2 * b, 0:128].rearrange("p (g t) -> p g t", g=2), ACT.Copy).then_inc(enc_hi, 1)
                act.wait_ge(enc_ps, 2 * b + 2)
                for s in range(2):
                    nc.scalar.activation(vencst[64 * s:64 * s + 64, b, :, 0:HD],
                                         ps[64 * s:64 * s + 64, 5 + 2 * b, :].rearrange("p (a e) -> p a e", e=HD), ACT.Copy).then_inc(enc_hi, 1)

            act.wait_ge(setup_done, 1)
            act.wait_ge(clo_done, B)
            act.wait_ge(count_done, 1)
            act.sem_inc(prj_c, 2)
            with act.Fori(0, CH) as c:
                for u in range(4):
                    act.wait_ge(prj_ps, c * 4 + (u + 1))
                    nc.scalar.activation(part_at(("qh", "kh")[u // 2], c, u % 2), ps[:, u, :], ACT.Copy).then_inc(prj_hi, 1)
            with act.Fori(0, TILES // 2) as it:
                for i in range(2):
                    for half in range(2):
                        act.wait_ge(v_ps, it * 4 + (2 * i + half + 1))
                        if half == 0:
                            act.wait_ge(v_stored[i], it * 16 + 16)
                        dst = vst[:, i, 4 * half:4 * half + 4].rearrange("p a (s v) -> p a s v", s=2)[:, :, :, 0:HD]
                        nc.scalar.activation(dst, ps[:, half, :].rearrange("p (a s e) -> p a s e", a=4, s=2),
                                             ACT.Copy).then_inc(v_hi, 1)
                    for half in range(2):
                        act.wait_ge(c_ps, it * 4 + (2 * i + half + 1))
                        nc.scalar.activation(sums_at(it, i, half),
                                             ps[:, 2 + half, :].rearrange("p (a s e) -> p a s e", a=4, s=2),
                                             ACT.Copy).then_inc(prj_c, 1)
            nc.scalar.preload_act_table(ACT.Square)
            with act.Fori(0, NP // PI) as it:
                for k in range(IU):
                    act.wait_ge(s_ready, it * IU + (k + 1))
                    act.wait_ge(av_done, it * IU + (k + 1))
                    nc.scalar.activation(A32[k % A_BUFS], Sb[k % S_BUFS], ACT.Square, bias=sqb[:, 0:1],
                                         scale=SQ_SCALE).then_inc(sq_done, 1)
            with act.Fori(0, BT) as t:
                for b in range(B):
                    act.wait_ge(at_ps, t * 2 + (b + 1) + 2)
                    act.wait_ge(o_ps, t * 2 + (b + 1))
                    nc.scalar.activation(aTh[b].rearrange("p a t -> p (a t)"), Sb[b], ACT.Copy).then_inc(at_hi, 1)
            stddev(2)
            hidden_hi(1)
            act.wait_ge(rt, 1)
            nc.scalar.activation(rk.rearrange("p t e -> p (t e)"), rk.rearrange("p t e -> p (t e)"), ACT.Exp).then_inc(exp_done, 1)
            nc.scalar.preload_act_table(ACT.Gelu_apprx_tanh)
            act.wait_ge(ld_k, 16 * 4)
            act.sem_inc(g_ok, PT)
            with act.Fori(0, CH) as c:
                for e in range(E):
                    act.wait_ge(dn_ps, c * E + (e + 1))
                    for pt in range(PT):
                        act.wait_ge(up_ps, c * (E * PT) + (e * PT + pt + 1))
                        nc.scalar.activation(G[e % 2][:, pt, :], ps[:, pt, :], ACT.Gelu_apprx_tanh,
                                             bias=b1s[:, e, pt:pt + 1]).then_inc(g_ok, 1)

        @block.vector
        def _(v):
            step = [0]

            def link(ins):
                step[0] += 1
                ins.then_inc(chain, 1)
                v.wait_ge(chain, step[0])

            v.wait_ge(ld_hc, 16)
            for n in range(NP):
                last = nc.vector.tensor_copy(C[:, n, :, :, HD], hc[:, :, None].to_broadcast([P, BT, 2]))
            last.then_inc(count_done, 1)
            v.wait_ge(silu_done, 1)
            nc.vector.tensor_copy(scb, scT[:, :, None].to_broadcast([P, B, P])).then_inc(scb_done, 1)

            def statistics(k):
                if k == 0:
                    for t in range(TILES):
                        if t % CT == 0:
                            v.wait_ge(ld_x[t // CT], 16)
                        nc.vector.bn_stats(stats[:, t, :], xs[:, t, :]).then_inc(st_done, 1)
                for t in range(TILES):
                    v.wait_ge(st_done, TILES * k + t + 1)
                    nc.vector.bn_aggr(mv[:, t, :], stats[:, t, :]).then_inc(agg_done, 1)
                v.wait_ge(agg_done, TILES * (k + 1))
                nc.vector.tensor_scalar(rs[:, 0, :], mv[:, :, 1], LN_EPS, None, ALU.add).then_inc(var_done, 1)
                v.wait_ge(var_done, k + 1)
                v.wait_ge(std_done, k + 1)
                link(nc.vector.reciprocal(rs[:, 2, :], rs[:, 1, :]))
                link(nc.vector.tensor_tensor(rs[:, 3, :], rs[:, 2, :], rs[:, 2, :], ALU.mult))
                link(nc.vector.tensor_tensor(rs[:, 3, :], rs[:, 3, :], rs[:, 0, :], ALU.mult))
                link(nc.vector.tensor_scalar(rs[:, 3, :], rs[:, 3, :], -0.5, 1.5, ALU.mult, ALU.add))
                link(nc.vector.tensor_tensor(rs[:, 2, :], rs[:, 2, :], rs[:, 3, :], ALU.mult))

            def normalise(k, dst):
                for t in range(TILES):
                    last = nc.vector.tensor_scalar(dst[:, t, :], xs[:, t, :], mv[:, t, 0:1], rs[:, 2, t:t + 1],
                                                   ALU.subtract, ALU.mult)
                    if t % CT == CT - 1:
                        last.then_inc(xn_done, 1)

            def modulate(k):
                for c in range(CH):
                    v.wait_ge(tr_done, CH * k + c + 1)
                    b = c // 2
                    nc.vector.tensor_scalar(hTf[:, 512 * c:512 * c + 512], ps[:, 4 + c % 2, :],
                                            modT[:, 2 * k + 1, b:b + 1], modT[:, 2 * k, b:b + 1],
                                            ALU.mult, ALU.add).then_inc(hTf_done, 1)

            def hidden_lo(k):
                with v.Fori(0, CH) as c:
                    v.wait_ge(hh_done, CH * k + c + 1)
                    nc.vector.tensor_tensor(hl[:, bass.ds(c * 512, 512)], hTf[:, bass.ds(c * 512, 512)],
                                            hh[:, bass.ds(c * 512, 512)], ALU.subtract).then_inc(hl_done, 1)

            statistics(0)
            normalise(0, xn)
            v.wait_ge(mod_ps, 1)
            nc.vector.tensor_copy(modT[:].rearrange("p m b -> p (m b)"), ps[:, 6, 0:8])
            link(nc.vector.tensor_copy(gate[:].rearrange("p m d -> p (m d)"), ps[:, 7, :]))
            v.sem_inc(mod_out, 1)
            for m in (1, 3):
                last = nc.vector.tensor_scalar(modT[:, m, :], modT[:, m, :], 1.0, None, ALU.add)
            link(last)
            link(nc.vector.tensor_scalar(gtmp, gate[:], 0.0, 2.0, ALU.is_ge, ALU.mult))
            link(nc.vector.scalar_tensor_tensor(out=gate[:], in0=gtmp, scalar=-1.0, in1=gate[:],
                                                op0=ALU.add, op1=ALU.mult))
            link(nc.vector.tensor_scalar(gate[:], gate[:], 0.25, None, ALU.max))
            link(nc.vector.scalar_tensor_tensor(out=gate[:], in0=gtmp, scalar=-1.0, in1=gate[:],
                                                op0=ALU.add, op1=ALU.mult))
            modulate(0)
            hidden_lo(0)
            for b in range(B):
                v.wait_ge(hTf_done, 2 * b + 2)
                nc.vector.tensor_tensor_scan(cums[b], hTf[:, N * b:N * b + N], hTf[:, N * b:N * b + N], 0.0,
                                             ALU.add, ALU.bypass).then_inc(scan_done, 1)
            for b in range(B):
                v.wait_ge(chi_done, b + 1)
                nc.vector.scalar_tensor_tensor(out=cl[:, N * b:N * b + N], in0=cums[b], scalar=0.5,
                                               in1=ch[:, N * b:N * b + N], op0=ALU.mult, op1=ALU.subtract).then_inc(clo_done, 1)
            for b in range(B):
                v.wait_ge(enc_hi, 4 * b + 2)
                for s in range(2):
                    last = nc.vector.tensor_tensor(kenc_sb[:, b, 1, s, :, 64 * s:64 * s + 64],
                                                   ps[:, 4 + 2 * b, 0:128].rearrange("p (g t) -> p g t", g=2),
                                                   kenc_sb[:, b, 0, s, :, 64 * s:64 * s + 64], ALU.subtract)
                last.then_inc(enc_lo, 1)
                v.wait_ge(enc_hi, 4 * b + 4)
                for s in range(2):
                    last = nc.vector.tensor_tensor(vencst[64 * s:64 * s + 64, b, :, HD + 1:2 * HD + 1],
                                                   ps[64 * s:64 * s + 64, 5 + 2 * b, :].rearrange("p (a e) -> p a e", e=HD),
                                                   vencst[64 * s:64 * s + 64, b, :, 0:HD], ALU.subtract)
                last.then_inc(enc_lo, 1)

            v.wait_ge(setup_done, 1)
            with v.Fori(0, CH) as c:
                for u in range(4):
                    v.wait_ge(prj_hi, c * 4 + (u + 1))
                    hi = part_at(("qh", "kh")[u // 2], c, u % 2)
                    lo = part_at(("ql", "kl")[u // 2], c, u % 2)
                    nc.vector.tensor_tensor(lo, ps[:, u, :], hi, ALU.subtract).then_inc(prj_out, 1)
            v.sem_inc(v_out, 2)
            with v.Fori(0, TILES // 2) as it:
                for i in range(2):
                    for half in range(2):
                        v.wait_ge(v_hi, it * 4 + (2 * i + half + 1))
                        pair = vst[:, i, 4 * half:4 * half + 4].rearrange("p a (s v) -> p a s v", s=2)
                        nc.vector.tensor_tensor(pair[:, :, :, HD + 1:2 * HD + 1],
                                                ps[:, half, :].rearrange("p (a s e) -> p a s e", a=4, s=2),
                                                pair[:, :, :, 0:HD], ALU.subtract).then_inc(v_out, 1)
            def low(it, k):
                if k % NU in POOL_LOW:
                    return
                if k % NU in MASKED or k % NU == 0:
                    n = sum(1 for j in range(k + 1) if j % NU in MASKED or j % NU == 0)
                    v.wait_ge(mk_done, it * (PI * (len(MASKED) + 1)) + n)
                else:
                    v.wait_ge(sq_done, it * IU + (k + 1))
                a = A32[k % A_BUFS]
                hi = a.bitcast(BF16).rearrange("p (n two) -> p n two", two=2)[:, :, 1]
                nc.vector.tensor_tensor(Alo[k % A_BUFS], a, hi, ALU.subtract).then_inc(lo_done, 1)

            def evacuate(it, k):
                v.wait_ge(av_done, it * IU + (k + 1 + A_BUFS))
                for s, half in DONE_AFTER[k % NU]:
                    acc_c = C[:, bass.ds(it * PI + k // NU, 1), 4 * half:4 * half + 4, s, :].rearrange("p a t e -> p (a t) e")
                    y = ps[:, 4 + 2 * s + half, 0:4 * (HD + 1)].rearrange("p (t e) -> p t e", t=4)
                    nc.vector.tensor_tensor(acc_c, y, acc_c, ALU.add).then_inc(y_free, 1)

            v.sem_inc(y_free, 4)
            with v.Fori(0, NP // PI) as it:
                for k in range(IU):
                    low(it, k)
                    if k >= 2 and (k - 2) % NU in DONE_AFTER:
                        evacuate(it, k - 2)
                evacuate(it, IU - 1)

            v.sem_inc(at_lo, 2)
            v.sem_inc(g_done, 2)
            v.wait_ge(y_free, 4 * NP + 4)
            nc.vector.tensor_scalar(zr[:], C[:, :, :, :, HD], EPS, None, ALU.add).then_inc(z0, 1)
            v.wait_ge(z0, 1)
            nc.vector.reciprocal(zr[:], zr[:]).then_inc(z_done, 1)
            with v.Fori(0, BT) as t:
                for b in range(B):
                    v.wait_ge(at_hi, t * 2 + (b + 1))
                    nc.vector.tensor_tensor(aTl[b].rearrange("p a t -> p (a t)"), Sb[b], aTh[b].rearrange("p a t -> p (a t)"),
                                            ALU.subtract).then_inc(at_lo, 1)
                for b in range(B):
                    xt = xs[:, bass.ds(t + BT * b, 1), :].rearrange("p a d -> p (a d)")
                    v.wait_ge(o_ps, t * 2 + (b + 1) + 2)
                    nc.vector.tensor_tensor(tmp[b], ps[:, 4 + b, 0:D], gate[:, b, :], ALU.mult).then_inc(g_done, 1)
                    v.wait_ge(g_done, t * 2 + (b + 1) + 2)
                    nc.vector.tensor_tensor(xt, xt, tmp[b], ALU.add).then_inc(x1_done, 1)
                    v.wait_ge(x1_done, t * 2 + (b + 1))
                    nc.vector.bn_stats(stats[:, bass.ds(t + BT * b, 1), :].rearrange("p a d -> p (a d)"), xt).then_inc(st_done, 1)
            statistics(1)
            normalise(1, xn2)
            modulate(1)
            hidden_lo(1)
            v.wait_ge(ld_k, 16 * 4)
            v.wait_ge(sc_ps, CH)
            every = lambda ap: ap[:, :, None].to_broadcast([P, TILES, E])
            orders = order[:, None, :].to_broadcast([P, TILES, E])
            link(nc.vector.tensor_tensor(sco, ps[:, 6, 0:TILES * E].rearrange("p (t e) -> p t e", e=E),
                                         brs[:, None, :].to_broadcast([P, TILES, E]), ALU.add))

            def pick(scores, chosen, peak):
                link(nc.vector.tensor_reduce(out=peak, in_=scores, axis=AX.X, op=ALU.max))
                link(nc.vector.tensor_tensor(cand, scores, every(peak), ALU.is_equal))
                link(nc.vector.tensor_tensor(cand, cand, orders, ALU.mult))
                link(nc.vector.tensor_reduce(out=mx[:], in_=cand, axis=AX.X, op=ALU.max))
                link(nc.vector.tensor_tensor(chosen, cand, every(mx[:]), ALU.is_equal))

            pick(sco, best, top[:, 0])
            nc.vector.tensor_tensor(rk, sco, every(top[:, 0]), ALU.subtract).then_inc(rt, 1)
            link(nc.vector.scalar_tensor_tensor(out=sco, in0=best, scalar=-3e38, in1=sco, op0=ALU.mult, op1=ALU.add))
            pick(sco, second, top[:, 1])
            link(nc.vector.tensor_tensor(best, best, second, ALU.add))
            v.wait_ge(exp_done, 1)
            link(nc.vector.tensor_tensor(rk, rk, best, ALU.mult))
            link(nc.vector.tensor_reduce(out=mx[:], in_=rk, axis=AX.X, op=ALU.add))
            link(nc.vector.reciprocal(mx[:], mx[:]))
            v.wait_ge(wts_zeroed, 1)
            nc.vector.tensor_tensor(wts[:, :, 0:E], rk, every(mx[:]), ALU.mult).then_inc(w_ready, 1)
            v.wait_ge(w_ready, 1)
            v.sem_inc(dn_free, 2)
            v.sem_inc(b2_read, 1)
            with v.Fori(0, CH) as c:
                def accumulate(e):
                    v.wait_ge(dn_ps, c * E + (e + 1) + 2)
                    v.wait_ge(dn_free, c * E + (e + 2))
                    for i in range(CT):
                        at = acc[:, bass.ds(c * CT + i, 1), :].rearrange("p a d -> p (a d)")
                        y = ps[:, 4 + e % 2, i * D:(i + 1) * D]
                        weight = wts[:, bass.ds(c * CT + i, 1), e:e + 1].rearrange("p a b -> p (a b)")
                        if e == 0:
                            last = nc.vector.tensor_scalar(at, y, weight, None, ALU.mult)
                        else:
                            last = nc.vector.scalar_tensor_tensor(out=at, in0=y, scalar=weight, in1=at,
                                                                  op0=ALU.mult, op1=ALU.add)
                    last.then_inc(dn_free, 1)

                for e in range(E):
                    for j in range(2):
                        v.wait_ge(g_ok, c * (E * PT) + (e * PT + 2 * j + 2 + PT))
                        g = G[e % 2][:, 2 * j:2 * j + 2, :]
                        hi = g.bitcast(BF16).rearrange("p a (n two) -> p a n two", two=2)[:, :, :, 1]
                        nc.vector.tensor_tensor(Glo[e % 2][:, 2 * j:2 * j + 2, :], g, hi, ALU.subtract).then_inc(glo, 1)
                    if e == 0:
                        nc.vector.tensor_copy(wc, wts[:, bass.ds(c * CT, CT), :]).then_inc(wc_done, 1)
                    if e == 1:
                        v.wait_ge(wt_ps, c + 1)
                        nc.vector.tensor_copy(wT, ps[:, 6, 0:P]).then_inc(wt_done, 1)
                    if e:
                        accumulate(e - 1)
                accumulate(E - 1)
                v.wait_ge(dn_free, c * E + (E + 2))
                at = acc[:, bass.ds(c * CT, CT), :]
                row = gate[:, bass.ds(c // 2 + 2, 1), :].to_broadcast([P, CT, D])
                v.wait_ge(b2_ps, c + 1)
                nc.vector.tensor_tensor(at, at, ps[:, 7, :].rearrange("p (i d) -> p i d", d=D), ALU.add).then_inc(b2_read, 1)
                v.wait_ge(b2_read, c + 2)
                nc.vector.tensor_tensor(at, at, row, ALU.mult).then_inc(fstep, 1)
                v.wait_ge(fstep, c + 1)
                nc.vector.tensor_tensor(at, at, xs[:, bass.ds(c * CT, CT), :], ALU.add).then_inc(fin_done, 1)

        @block.tensor
        def _(pe):
            mm = nc.tensor.matmul

            def three(dst, sh, sl, mh, ml):
                mm(dst, sh, mh, start=True, stop=False)
                mm(dst, sh, ml, start=False, stop=False)
                return mm(dst, sl, mh, start=False, stop=True)

            def router(c):
                pe.wait_ge(hTf_done, CH + c + 1)
                for t in range(CT * c, CT * (c + 1)):
                    last = mm(ps[:, 6, E * t:E * (t + 1)], hTf[:, P * t:P * (t + 1)], wrs[:], start=True, stop=True)
                last.then_inc(sc_ps, 1)

            def transposes(k, src):
                for c in range(CH):
                    if k == 1 and c >= 2:
                        router(c - 2)
                    pe.wait_ge(xn_done, CH * k + c + 1)
                    if c >= 2:
                        pe.wait_ge(hTf_done, CH * k + c - 1)
                    for i in range(CT):
                        last = nc.tensor.transpose(ps[:, 4 + c % 2, i * P:(i + 1) * P], src[:, CT * c + i, :], id32[:])
                    last.then_inc(tr_done, 1)

            pe.wait_ge(ld_wm, 16)
            pe.wait_ge(silu_done, 1)
            for m, col in enumerate((0, 1, 3, 4)):
                mm(ps[:, 6, 2 * m:2 * m + 2], wms[:, col * D:(col + 1) * D], scT[:], start=True, stop=True)
            pe.wait_ge(scb_done, 1)
            for m, col in enumerate((2, 5)):
                for b in range(B):
                    last = mm(ps[:, 7, (2 * m + b) * D:(2 * m + b + 1) * D], scb[:, b, :], wms[:, col * D:(col + 1) * D],
                              start=True, stop=True)
            last.then_inc(mod_ps, 1)
            pe.wait_ge(ld_id, 16)
            transposes(0, xn)

            pe.wait_ge(wa_lo, 1)
            pe.wait_ge(hl_done, CH)
            pe.wait_ge(mod_out, 1)
            pe.wait_ge(hTf_done, CH)
            for b in range(B):
                t = slice(N * b, N * b + ENC)
                for g in range(2):
                    w = slice(KE0 + P * g, KE0 + P * (g + 1))
                    last = three(ps[:, 4 + 2 * b, ENC * g:ENC * (g + 1)], wah[:, w], wal[:, w], hh[:, t], hl[:, t])
                last.then_inc(enc_ps, 1)
                for s in range(2):
                    w = slice(VE0 + 512 * s, VE0 + 512 * (s + 1))
                    last = three(ps[64 * s:64 * s + 64, 5 + 2 * b, :], hh[:, t], hl[:, t], wah[:, w], wal[:, w])
                last.then_inc(enc_ps, 1)
            for u in range(4):
                w = Q0 + P * u
                three(ps[:, u, :], wah[:, w:w + P], wal[:, w:w + P], hh[:, 0:512], hl[:, 0:512]).then_inc(prj_ps, 1)
            with pe.Fori(1, CH) as c:
                for u in range(4):
                    pe.wait_ge(prj_out, c * 4 + (u + 1 - 4))
                    w = Q0 + P * u
                    three(ps[:, u, :], wah[:, w:w + P], wal[:, w:w + P],
                          hh[:, bass.ds(c * 512, 512)], hl[:, bass.ds(c * 512, 512)]).then_inc(prj_ps, 1)
            pe.wait_ge(prj_out, 4 * CH)
            pe.wait_ge(clo_done, B)
            with pe.Fori(0, TILES // 2) as it:
                for i in range(2):
                    for xh, xl, bank0, free, done in ((hh, hl, 0, v_out, v_ps), (ch, cl, 2, prj_c, c_ps)):
                        for half in range(2):
                            w = V0 + 512 * half
                            pe.wait_ge(free, it * 4 + (2 * i + half + 1))
                            three(ps[:, bank0 + half, :], xh[:, bass.ds(it * 2 * P + P * i, P)],
                                  xl[:, bass.ds(it * 2 * P + P * i, P)],
                                  wah[:, w:w + 512], wal[:, w:w + 512]).then_inc(done, 1)
            def scores(it, k):
                hf, unit = (k // NU) % 2, UNITS[k % NU]
                if k % NU == 0:
                    pe.wait_ge(slot[hf], it * (112 * PI // 2) + 112 * (1 + k // (2 * NU)))
                if k >= S_BUFS:
                    pe.wait_ge(sq_done, it * IU + (k + 1 - S_BUFS))
                for off, w, s, j, q0 in unit:
                    col = 2 * N if j == "enc" else N * s + P * j
                    last = mm(Sb[k % S_BUFS][:, off:off + w], kS[hf][:, col:col + P], qS[hf][:, q0:q0 + w], start=True, stop=True)
                last.then_inc(s_ready, 1)

            def products(hf, k, blocks, first):
                a = A32[k % A_BUFS]
                hi = a.bitcast(BF16).rearrange("p (n two) -> p n two", two=2)[:, :, 1]
                for n, (off, s, j, i) in enumerate(blocks):
                    y = ps[:, 4 + 2 * s + i // 4, (i % 4) * (HD + 1):(i % 4 + 1) * (HD + 1)]
                    t = VW * (2 * (BT if j == "enc" else j) + s)
                    vv = vS[hf][:, t:t + VW]
                    one = dict(start=False, stop=True, skip_group_check=True)
                    mm(y, hi[:, off:off + P], vv[:, 0:HD + 1], start=first and n == 0, stop=True, skip_group_check=True)
                    mm(y[:, 0:HD], hi[:, off:off + P], vv[:, HD + 1:2 * HD + 1], **one)
                    last = mm(y, Alo[k % A_BUFS][:, off:off + P], vv[:, 0:HD + 1], **one)
                return last

            def weighted(it, k):
                j, hf, kk = k // NU, k // NU % 2, k % NU
                by_pool = sum(1 for j in range(k + 1) if j % NU in POOL_LOW)
                if kk in POOL_LOW:
                    pe.wait_ge(lo_pool, it * (PI * len(POOL_LOW)) + by_pool)
                else:
                    pe.wait_ge(lo_done, it * (PI * (NU - len(POOL_LOW))) + (k + 1 - by_pool))
                if kk == 0:
                    for n, (s, half) in enumerate(GROUPS[:3]):
                        pe.wait_ge(y_free, it * (4 * PI) + (4 * j + n + 1))
                        products(hf, k, [(512 * half + P * m, s, "enc", 4 * half + m) for m in range(4)], True)
                    return
                blocks = [(off + P * m, s, key, q0 // P + m) for off, w, s, key, q0 in UNITS[kk] for m in range(w // P)]
                last = products(hf, k, blocks, False)
                if kk == 1:
                    s, half = GROUPS[3]
                    pe.wait_ge(y_free, it * (4 * PI) + (4 * j + 4))
                    last = products(hf, k - 1, [(512 * half + P * m, s, "enc", 4 * half + m) for m in range(4)], True)
                last.then_inc(av_done, 2 if kk == 1 else 1)

            pe.wait_ge(prj_c, 2 * TILES + 2)
            pe.sem_inc(av_done, A_BUFS)
            for k in range(LAG):
                scores(0, k)
            with pe.Fori(0, NP // PI - 1) as it:
                for k in range(IU):
                    scores(it, k + LAG)
                    weighted(it, k)
            for k in range(IU):
                if k + LAG < IU:
                    scores(NP // PI - 1, k + LAG)
                weighted(NP // PI - 1, k)

            pe.sem_inc(at_ps, 2)
            pe.sem_inc(o_ps, 2)
            with pe.Fori(0, BT) as t:
                for b in range(B):
                    pe.wait_ge(an_done, t * 2 + (b + 1))
                    pe.wait_ge(at_lo, t * 2 + (b + 1))
                    for p in range(PAIRS):
                        last = nc.tensor.transpose(Sb[b][:, P * p:P * (p + 1)],
                                                   an[b][:, 2 * p:2 * p + 2, :].rearrange("p s e -> p (s e)"), id32[:])
                    last.then_inc(at_ps, 1)
                for b in range(B):
                    pe.wait_ge(at_lo, t * 2 + (b + 1) + 2)
                    pe.wait_ge(g_done, t * 2 + (b + 1))
                    bank = ps[:, 4 + b, 0:D]
                    for p in range(PAIRS):
                        w = slice(O0 + D * p, O0 + D * (p + 1))
                        mm(bank, aTh[b][:, p, :], wah[:, w], start=p == 0, stop=False)
                        mm(bank, aTh[b][:, p, :], wal[:, w], start=False, stop=False)
                        last = mm(bank, aTl[b][:, p, :], wah[:, w], start=False, stop=p == PAIRS - 1)
                    last.then_inc(o_ps, 1)

            pe.wait_ge(ld_k, 16 * 4)
            transposes(1, xn2)
            router(2)
            router(3)

            pe.wait_ge(ff_split, 4)
            pe.wait_ge(ld_b2, 16 * 4)
            pe.sem_inc(dn_ps, 2)

            with pe.Fori(0, CH) as c:
                def up(e):
                    for pt in range(PT):
                        pe.wait_ge(g_ok, c * (E * PT) + (e * PT + pt + 1))
                        w = slice(P * pt, P * (pt + 1))
                        three(ps[:, pt, :], w1h[:, e, w], w1l[:, e, w], hh[:, bass.ds(c * 512, 512)],
                              hl[:, bass.ds(c * 512, 512)]).then_inc(up_ps, 1)

                def down(e):
                    pe.wait_ge(dn_free, c * E + (e + 1))
                    pe.wait_ge(glo, c * (2 * E) + (2 * e + 2))
                    hi = G[e % 2].bitcast(BF16).rearrange("p a (n two) -> p a n two", two=2)[:, :, :, 1]
                    for i in range(CT):
                        bank, t = ps[:, 4 + e % 2, i * D:(i + 1) * D], slice(P * i, P * (i + 1))
                        for pt in range(PT):
                            mm(bank, hi[:, pt, t], w2h[:, e, pt, :], start=pt == 0, stop=False)
                            mm(bank, hi[:, pt, t], w2l[:, e, pt, :], start=False, stop=False)
                            last = mm(bank, Glo[e % 2][:, pt, t], w2h[:, e, pt, :], start=False, stop=pt == PT - 1)
                    last.then_inc(dn_ps, 1)

                pe.wait_ge(hl_done, c + (CH + 1))
                up(0)
                for e in range(1, E):
                    up(e)
                    if e == 1:
                        pe.wait_ge(wc_done, c + 1)
                        nc.tensor.transpose(ps[:, 6, 0:P], wc.rearrange("p t e -> p (t e)"), id32[:]).then_inc(wt_ps, 1)
                    elif e == 2:
                        pe.wait_ge(wt_done, c + 1)
                        pe.wait_ge(b2_read, c + 1)
                        mm(ps[:, 7, :], wT, b2s.rearrange("p i d -> p (i d)"), start=True, stop=True).then_inc(b2_ps, 1)
                    down(e - 1)
                down(E - 1)


def kernel(L0_attn_x, L0_attn_Wq, L0_attn_Wk, L0_attn_Wv, L0_attn_Wk_enc, L0_attn_Wv_enc, L0_attn_Wout,
           L0_ffn_W1, L0_ffn_b1, L0_ffn_W2, L0_ffn_b2, L0_ffn_Wr, L0_ffn_br, L0_c, L0_wmod):
    import numpy as np
    import concourse.bacc as bacc
    from concourse.bass_utils import run_bass_kernel_spmd

    a = np.asarray

    def groups(w):
        return a(w).reshape(4, 2, 2, FD, D).transpose(4, 1, 2, 0, 3).reshape(D, 256)

    wo = a(L0_attn_Wout).T.reshape(PAIRS, P, D).transpose(1, 0, 2).reshape(P, PAIRS * D)
    ve = a(L0_attn_Wv_enc).reshape(PAIRS, 2, HD, D).transpose(3, 1, 0, 2).reshape(D, H * HD)
    arrays = {
        "x": a(L0_attn_x).reshape(TILES, P, D),
        "wqkT": np.concatenate([groups(L0_attn_Wq), groups(L0_attn_Wk), groups(L0_attn_Wk_enc)], axis=1),
        "wvT": np.concatenate([a(L0_attn_Wv).T, ve], axis=1),
        "woT": wo,
        "w1": a(L0_ffn_W1).transpose(1, 0, 2).reshape(D, E * PF),
        "b1T": a(L0_ffn_b1).reshape(E, PT, P).transpose(2, 0, 1),
        "w2": a(L0_ffn_W2).reshape(E, PT, P, D).transpose(2, 0, 1, 3).reshape(P, E * PT * D),
        "b2": a(L0_ffn_b2),
        "wr": a(L0_ffn_Wr),
        "br": a(L0_ffn_br),
        "cT": a(L0_c).T,
        "wmod": a(L0_wmod),
        "ident": np.eye(P, dtype=np.float32),
        "half_count": (0.5 * (P * np.arange(BT)[None, :] + np.arange(P)[:, None] + 1)).astype(np.float32),
        "index_order": np.broadcast_to(E - np.arange(E, dtype=np.float32), (P, E)),
    }
    nc = bacc.Bacc("TRN2", target_bir_lowering=False, num_devices=1)
    args = {}
    feed = {}
    for name, value in arrays.items():
        feed[name + "_dram"] = np.ascontiguousarray(value)
        args[name] = nc.dram_tensor(name + "_dram", value.shape, F32, kind="ExternalInput").ap()
    out = nc.dram_tensor("out_dram", (TILES, P, D), F32, kind="ExternalOutput").ap()
    adaln_block(nc, out=out, **args)
    r = run_bass_kernel_spmd(nc, [feed], core_ids=[0])
    return r.results[0]["out_dram"].reshape(B, N, D)
```

```python
from contextlib import ExitStack

import concourse.bass as bass
from concourse import mybir

F32 = mybir.dt.float32
F16 = mybir.dt.float16
BF16 = mybir.dt.bfloat16
ACT = mybir.ActivationFunctionType
ALU = mybir.AluOpType
AX = mybir.AxisListType

P = 128
B, N, D = 2, 1024, 128
H, FD, HD = 16, 16, 64
ENC = 64
E, PF = 8, 512
PT = PF // P
TILES = B * N // P
BT = N // P
PAIRS = H // 2
NP = B * PAIRS
CH = 4
CT = TILES // CH
VW = 130
VROW = 2 * (BT + 1) * VW
EPS = 1e-12
LN_EPS = 1e-5
SQ_SCALE = 0.25 * 2.0 ** -0.5
SQ_BIAS = 2.0 ** -0.5
A_BUFS = 5
S_BUFS = 2
LAG = 4
PI = 4

def _units():
    first = lambda s: [(0, 512, s, 0, 0), (512, 384, s, 1, 128), (896, 128, s, 3, 384)]
    full = lambda s, j: [(0, 512, s, j, 512), (512, 512, s, j + 1, 512)]
    last = lambda s: [(0, 512, s, 4, 512), (512, 384, s, 5, 640), (896, 128, s, 7, 896)]
    mid = [(0, 256, 0, 2, 256), (256, 256, 0, 6, 768), (512, 256, 1, 2, 256), (768, 256, 1, 6, 768)]
    enc = [(0, 512, None, "enc", 0), (512, 512, None, "enc", 512)]
    return [enc, first(0), first(1), mid, full(0, 0), full(0, 2), last(0), full(1, 0), full(1, 2), last(1)]


UNITS = _units()
NU = len(UNITS)
IU = PI * NU
MASKED = (1, 2, 3, 6, 9)
POOL_LOW = (4, 7)
DONE_AFTER = {3: [(0, 0), (1, 0)], 6: [(0, 1)], 9: [(1, 1)]}
GROUPS = [(0, 0), (1, 0), (0, 1), (1, 1)]


def adaln_block(nc, x, wqkT, wvT, woT, w1, b1T, w2, b2, wr, br, cT, wmod, ident, half_count, index_order, out):
    ctx = ExitStack()
    with ctx:
        def sb(name, shape, dt):
            return ctx.enter_context(nc.sbuf_tensor(name, shape, dt))

        def sem(name):
            return ctx.enter_context(nc.semaphore(name))

        xs = sb("xs", [P, TILES, D], F32)
        hTf = sb("hTf", [P, TILES * P + 32], F32)
        hh = sb("hh", [P, TILES * P], F16)
        hl = sb("hl", [P, TILES * P], F16)
        ch = sb("ch", [P, TILES * P], F16)
        cl = sb("cl", [P, TILES * P], F16)
        WA = 3 * 256 + 3 * 1024
        wah = sb("wah", [P, WA], F16)
        wal = sb("wal", [P, WA], F16)
        Q0, K0, KE0, V0, VE0, O0 = 0, 256, 512, 768, 768 + 1024, 768 + 2048
        w1h = sb("w1h", [P, E, PF], F16)
        w1l = sb("w1l", [P, E, PF], F16)
        w2h = sb("w2h", [P, E, PT, D], F16)
        w2l = sb("w2l", [P, E, PT, D], F16)
        C = sb("C", [P, NP, BT, 2, HD + 1], F32)
        vst = sb("vst", [P, 2, PAIRS, 2 * VW], F16)
        id32 = sb("id32", [P, P], F32)
        arena = sb("arena", [P, 49152 // 4], F32)

        def view(byte, shape, dt):
            n = 1
            for s in shape:
                n *= s
            size = n * (4 if dt == F32 else 2)
            a = arena[:, byte // 4:(byte + size) // 4]
            if dt != F32:
                a = a.bitcast(dt)
            if len(shape) > 1:
                names = "abcd"[:len(shape)]
                a = a.rearrange(f"p ({' '.join(names)}) -> p {' '.join(names)}",
                                **{n_: s for n_, s in zip(names, shape)})
            return a

        xn = view(0, [TILES, D], F32)
        wst = view(8192, [WA], F32)
        wms = view(8192 + WA * 4, [6 * D], F32)
        cums = [view(4 * N * b, [N], F32) for b in range(B)]
        ffs1 = view(32768, [E * PF], F32)
        ffs2 = C[:, PAIRS:NP].rearrange("p n t s e -> p (n t s e)")[:, 0:E * PF]
        plain = {n_: view(8192 * i, [B, 2, N], F16) for i, n_ in enumerate(("qh", "ql", "kh", "kl"))}
        A32 = [view(4096 * i, [1024], F32) for i in range(4)] + [ch[:].bitcast(F32)]
        Alo = [view(16384 + 2048 * i, [1024], F16) for i in range(4)] + [cl[:, 0:1024]]
        SLOT = 2 * (N + 2 * N + P + VROW)
        SLOT0 = 49152 - 1024 - 2 * SLOT
        qS = [view(SLOT0 + SLOT * i, [N], F16) for i in range(2)]
        kS = [view(SLOT0 + SLOT * i + 2 * N, [2 * N + P], F16) for i in range(2)]
        vS = [view(SLOT0 + SLOT * i + 2 * (3 * N + P), [VROW], F16) for i in range(2)]
        def heads(ap):
            return ap.rearrange("p (a s v) -> p a s v", a=PAIRS, s=2)

        V_BUFS = 4
        own = vst[:].rearrange("p i a v -> p i (a v)")
        v_st = [heads(vS[1][:, 0:2 * VW * PAIRS]), heads(hTf[:, N:N + VW * PAIRS].bitcast(F16)), heads(own[:, 0]), heads(own[:, 1])]
        an = [view(4096 * i, [H, HD], F32) for i in range(2)]
        anl = [view(20480 + 2048 * i, [H, HD], F16) for i in range(2)]
        aTh = [view(8192 + 2048 * i, [PAIRS, P], BF16) for i in range(2)]
        aTl = [view(12288 + 2048 * i, [PAIRS, P], F16) for i in range(2)]
        id16 = view(19456, [P], F16)
        idb16 = view(19712, [P], BF16)
        tmp = [view(16384 + 512 * i, [D], F32) for i in range(2)]
        xn2 = view(24576, [TILES, D], F32)
        G = [view(8192 * i, [PT, 512], F32) for i in range(2)]
        Glo = [view(16384 + 4096 * i, [PT, 512], F16) for i in range(2)]
        acc = view(32768, [TILES, D], F32)

        kenc_sb = hTf[:, 0:N].bitcast(F16).rearrange("p (b c s g t) -> p b c s g t", b=B, c=2, s=2, g=2)
        kenc = [[[kenc_sb[:, b, part, s] for s in range(2)] for part in range(2)] for b in range(B)]
        vencst = sb("vencst", [P, B, PAIRS, VW], F16)
        stats = view(31744, [TILES, 6], F32)
        mv = sb("mv", [P, TILES, 2], F32)
        rs = sb("rs", [P, 4, TILES], F32)
        cs = sb("cs", [P, B], F32)
        scT = sb("scT", [P, B], F32)
        scb = view(30720, [B, P], F32)
        modT = sb("modT", [P, 4, B], F32)
        gate = sb("gate", [P, 4, P], F32)
        gtmp = view(22528, [4, P], F32)
        hc = sb("hc", [P, BT], F32)
        sqb = sb("sqb", [P, 1], F32)
        zr = view(18432, [NP, BT, 2], F32)
        wrs = sb("wrs", [P, E], F32)
        wrh = sb("wrh", [P, E], F16)
        wrl = sb("wrl", [P, E], F16)
        brs = sb("brs", [P, E], F32)
        b1s = sb("b1s", [P, E, PT], F32)
        b2s = view(45056, [4, D], F32)
        sco = view(24576, [TILES, E], F32)
        rk = view(25088, [TILES, E], F32)
        cand = view(25600, [TILES, E], F32)
        best = view(26112, [TILES, E], F32)
        second = view(26624, [TILES, E], F32)
        top = view(27136, [2, TILES], F32)
        order = sb("order", [P, E], F32)
        mx = sb("mx", [P, TILES], F32)
        wts = view(40960, [TILES, 32], F32)
        wT = view(43008, [P], F32)
        wc = view(43520, [4, 32], F32)

        ps = ctx.enter_context(nc.psum_tensor("ps", [P, 8, 512], F32))
        Sb = [ps[:, 2 * i:2 * i + 2, :].rearrange("p a b -> p (a b)") for i in range(2)]

        sQ = nc.dram_tensor("scratch_q", [B, P, PAIRS, N], F16, kind="Internal").ap()
        sK = nc.dram_tensor("scratch_k", [B, P, PAIRS, N], F16, kind="Internal").ap()
        sKE = nc.dram_tensor("scratch_k_enc", [B, P, PAIRS, P], F16, kind="Internal").ap()
        sV = nc.dram_tensor("scratch_v", [NP, P, VROW], F16, kind="Internal").ap()

        ld_c = sem("c_loaded")
        ld_hc = sem("half_counts_loaded")
        ld_x = [sem(f"x_loaded{q}") for q in range(CH)]
        ld_wm = sem("wmod_loaded")
        ld_id = sem("identity_loaded")
        ld_wa = sem("attn_weights_loaded")
        ld_w1 = sem("w1_loaded")
        ld_w2 = sem("w2_loaded")
        ld_k = sem("consts_loaded")
        ld_b2 = sem("b2_loaded")
        silu_done = sem("silu_done")
        scb_done = sem("silu_broadcast")
        mod_ps = sem("mod_products")
        mod_out = sem("modulation_banks_read")
        modT_done = sem("modT_done")
        wa_hi = sem("wa_hi")
        wa_lo = sem("wa_lo")
        ff_split = sem("ffn_split")
        setup_done = sem("setup_done")
        kenc_zero = sem("kenc_zeroed")
        slot_zeroed = sem("slots_zeroed")
        v_columns = sem("constant_columns_of_v")
        count_done = sem("half_counts_in_C")
        wts_zeroed = sem("wts_zeroed")
        b2_zeroed = sem("b2_blocks_zeroed")
        st_done = sem("bn_stats_done")
        agg_done = sem("bn_aggr_done")
        var_done = sem("var_plus_eps")
        std_done = sem("std_done")
        xn_done = sem("xn_done")
        tr_done = sem("transposed")
        hTf_done = sem("hTf_done")
        hTf_act = sem("hTf_done_by_act")
        hh_done = sem("hh_done")
        hl_done = sem("hl_done")
        scan_done = sem("scan_done")
        chi_done = sem("cum_hi")
        clo_done = sem("cum_lo")
        enc_ps = sem("enc_products")
        enc_hi = sem("enc_hi")
        enc_lo = sem("enc_lo")
        enc_stored = sem("encoder_stored")
        prj_ps = sem("projection_products")
        prj_hi = sem("projection_hi")
        prj_out = sem("projection_out")
        stacked = [sem("stacked_batch0"), sem("stacked_batch1")]
        v_ps = sem("v_products")
        v_hi = sem("v_hi")
        v_out = sem("v_out")
        v_stored = [sem(f"v_stored{i}") for i in range(4)]
        c_ps = sem("running_sum_products")
        prj_c = sem("running_sums_out")
        slot = [sem("slot0_loaded"), sem("slot1_loaded")]
        s_ready = sem("scores_ready")
        sq_done = sem("squared")
        mk_done = sem("masked")
        lo_done = sem("a_lo_done")
        lo_pool = sem("a_lo_done_by_pool")
        av_done = sem("a_buffers_free_and_units_done")
        y_free = sem("y_bank_free")
        z0 = sem("den_ready")
        z_done = sem("z_done")
        an_done = sem("normalized")
        anl_done = sem("attn_lo_done")
        at_ps = sem("attn_transposed")
        at_copied = sem("attnT_copied")
        o_ps = sem("out_products")
        g_done = sem("gated")
        x1_done = sem("x1_done")
        sc_ps = sem("router_products")
        rt = sem("router_step")
        exp_done = sem("exp_done")
        w_ready = sem("expert_weights_ready")
        up_ps = sem("up_products")
        g_ok = sem("gelu_done")
        glo = sem("gelu_lo")
        dn_ps = sem("down_products")
        dn_free = sem("down_bank_free")
        wc_done = sem("chunk_weights_copied")
        wt_ps = sem("weights_transposed")
        wt_done = sem("wT_done")
        b2_ps = sem("b2_products")
        b2_read = sem("b2_part_read")
        fstep = sem("final_step")
        fin_done = sem("final_done")
        out_done = sem("out_stored")
        chain = sem("vector_chain")
        pool_turn = sem("pool_turn")

        def part_at(name, c, g):
            return plain[name][:, bass.ds(c // 2, 1), g, bass.ds((c % 2) * 512, 512)].rearrange("p a t -> p (a t)")

        def sums_at(it, i, half):
            at = C[:, bass.ds((it // (BT // 4)) * PAIRS + 4 * half, 4), bass.ds((it % (BT // 4)) * 4 + i, 1), :, 0:HD]
            return at.rearrange("p n a s e -> p (n a) s e")

        def half_counts(engine, n0, n1):
            for n in range(n0, n1):
                last = engine.tensor_copy(C[:, n, :, :, HD], hc[:, :, None].to_broadcast([P, BT, 2]))
            return last

        def store_stack(engine, b, names):
            for name in names:
                dst, rows = {"qh": (sQ, (0, 2)), "ql": (sQ, (1, 3)), "kh": (sK, (0, 1)), "kl": (sK, (2, 3))}[name]
                for s in range(2):
                    for r in rows:
                        to = dst[b, 64 * s + 16 * r:64 * s + 16 * r + 16].rearrange("i (k g) t -> k i (g t)", g=2)
                        engine.dma_start(to, plain[name][64 * s:64 * s + 64, b].rearrange("p g t -> p (g t)"))\
                              .then_inc(stacked[b], 16)

        block = ctx.enter_context(nc.Block())

        @block.sync
        def _(sp):
            sp.dma_start(cs[:], cT).then_inc(ld_c, 16)
            sp.dma_start(hc[:], half_count).then_inc(ld_hc, 16)
            for q in range(4):
                sp.dma_start(xs[:, CT * q:CT * q + CT, :],
                             x[CT * q:CT * q + CT].rearrange("t p d -> p t d")).then_inc(ld_x[q], 16)
            sp.dma_start(wms, wmod).then_inc(ld_wm, 16)
            sp.dma_start(id32[:], ident).then_inc(ld_id, 16)
            sp.dma_start(wst[:, 0:V0], wqkT).then_inc(ld_wa, 16)
            sp.dma_start(wst[:, V0:O0], wvT).then_inc(ld_wa, 16)
            sp.dma_start(wst[:, O0:WA], woT).then_inc(ld_wa, 16)
            sp.dma_start(ffs1, w1).then_inc(ld_w1, 16)
            sp.dma_start(ffs2, w2).then_inc(ld_w2, 16)
            for dst, src in ((wrs[:], wr), (b1s[:], b1T), (order[:], index_order)):
                sp.dma_start(dst, src).then_inc(ld_k, 16)
            sp.dma_start(brs[:], br.partition_broadcast(P)).then_inc(ld_k, 16)
            def store_v(t):
                sp.wait_ge(v_out, 2 * (t + 1) + 2)
                b, at = t // BT, 2 * VW * (t % BT)
                sp.dma_start(sV[PAIRS * b:PAIRS * (b + 1), :, at:at + 2 * VW].rearrange("n p v -> p n v"),
                             v_st[t % V_BUFS].rearrange("p a s v -> p a (s v)")).then_inc(v_stored[t % V_BUFS], 16)

            def store_encoder_keys(b, s, r):
                to = sKE[b, 64 * s + 16 * r:64 * s + 16 * r + 16].rearrange("i (k g) t -> k i (g t)", g=2)
                sp.dma_start(to, kenc[b][r // 2][s][64 * s:64 * s + 64].rearrange("p g t -> p (g t)")).then_inc(enc_stored, 16)

            def store_encoder_values(b, s):
                rows, col = slice(64 * s, 64 * s + 64), VW * (2 * BT + s)
                sp.dma_start(sV[PAIRS * b:PAIRS * (b + 1), rows, col:col + VW].rearrange("n p v -> p n v"),
                             vencst[rows, b]).then_inc(enc_stored, 16)

            def load(n, hf):
                lo, hi, V2 = slice(0, 64), slice(64, P), 2 * VW * BT
                for dst, src, rows in ((qS[hf], sQ, slice(0, P)), (kS[hf][lo, 0:N], sK, lo), (kS[hf][hi, N:2 * N], sK, hi),
                                       (kS[hf][:, 2 * N:], sKE, slice(0, P))):
                    at = src[bass.ds(n // PAIRS, 1), rows, bass.ds(n % PAIRS, 1), :]
                    sp.dma_start(dst, at.rearrange("a p n t -> (a p) (n t)")).then_inc(slot[hf], 16)
                for rows, c0, c1 in ((slice(0, P), 0, V2), (lo, V2, V2 + VW), (hi, V2 + VW, V2 + 2 * VW)):
                    sp.dma_start(vS[hf][rows, c0:c1], sV[bass.ds(n, 1), rows, c0:c1].rearrange("a p t -> (a p) t"))\
                      .then_inc(slot[hf], 16)

            for i in range(V_BUFS):
                sp.sem_inc(v_stored[i], 16)
            sp.wait_ge(prj_out, 8)
            store_stack(sp, 0, ("qh", "ql", "kh", "kl"))
            sp.wait_ge(enc_lo, 2 * B)
            for t in range(TILES):
                if t == TILES - 4:
                    sp.wait_ge(enc_stored, 16 * B * (8 + 2))
                    sp.wait_ge(slot_zeroed, 2)
                    sp.wait_ge(stacked[0], 16 * 16)
                    for i in range(V_BUFS):
                        sp.wait_ge(v_stored[i], 16 * (BT // V_BUFS + 1))
                    load(0, 0)
                if t == TILES - 1:
                    sp.wait_ge(v_stored[0], 16 * (TILES // V_BUFS + 1))
                    load(1, 1)
                store_v(t)
                if t < BT:
                    store_encoder_keys(t // 4, t % 2, t // 2 % 2)
                    store_encoder_keys(t // 4, t % 2, t // 2 % 2 + 2)
                if 6 <= t < 6 + 4:
                    store_encoder_values((t - 6) // 2, (t - 6) % 2)
            sp.wait_ge(stacked[1], 16 * 16)
            for i in range(V_BUFS):
                sp.wait_ge(v_stored[i], 16 * (TILES // V_BUFS + 1))
            with sp.Fori(0, NP // 2 - 1) as it:
                for hf in range(2):
                    sp.wait_ge(av_done, it * (2 * NU) + (NU * (hf + 1) + A_BUFS))
                    load(it * 2 + (hf + 2), hf)
            sp.wait_ge(b2_zeroed, 1)
            for i in range(4):
                sp.dma_start(b2s[32 * i:32 * i + E, i, :], b2).then_inc(ld_b2, 16)
            with sp.Fori(0, CH) as c:
                sp.wait_ge(fin_done, c + 1)
                sp.dma_start(out[bass.ds(c * CT, CT)].rearrange("t p d -> p t d"), acc[:, bass.ds(c * CT, CT), :]).then_inc(out_done, 16)
            sp.wait_ge(out_done, 16 * CH)

        @block.gpsimd
        def _(gp):
            for hf in range(2):
                gp.memset(vst[:, hf].rearrange("p a (s v) -> p a s v", s=2)[:, :, :, HD:HD + 1], 1.0)
                gp.memset(vencst[:, hf, :, HD:HD + 1], 1.0)
                gp.memset(vencst[:, hf, :, VW - 1:VW], 0.0)
                gp.memset(vst[:, hf].rearrange("p a (s v) -> p a s v", s=2)[:, :, :, VW - 1:VW], 0.0)
            gp.memset(sqb[:], SQ_BIAS).then_inc(setup_done, 1)
            gp.wait_ge(wa_hi, 1)
            gp.tensor_tensor(wal[:], wst, wah[:], ALU.subtract).then_inc(wa_lo, 1)
            w1_parts = [w[:].rearrange("p e f -> p (e f)") for w in (w1h, w1l)]
            w2_parts = [w[:].rearrange("p e a d -> p (e a d)") for w in (w2h, w2l)]

            gp.wait_ge(scan_done, B)
            gp.wait_ge(hl_done, CH)
            gp.memset(hTf[:, 0:N], 0.0).then_inc(kenc_zero, 1)
            gp.wait_ge(ld_w1, 16)
            gp.tensor_scalar(w1_parts[0], ffs1, 1.0, 0.0, ALU.mult, ALU.add).then_inc(ff_split, 1)
            gp.wait_ge(ff_split, 1)
            gp.tensor_tensor(w1_parts[1], ffs1, w1_parts[0], ALU.subtract).then_inc(ff_split, 1)
            gp.wait_ge(ld_w2, 16)
            gp.tensor_scalar(w2_parts[0], ffs2, 1.0, 0.0, ALU.mult, ALU.add).then_inc(ff_split, 1)

            def zero_rows(hf):
                gp.memset(kS[hf][64:P, 0:N], 0.0)
                gp.memset(kS[hf][0:64, N:2 * N], 0.0)
                gp.memset(vS[hf][64:P, 2 * VW * BT:2 * VW * BT + VW], 0.0)
                return gp.memset(vS[hf][0:64, 2 * VW * BT + VW:VROW], 0.0)

            gp.wait_ge(ff_split, 3)
            zero_rows(1).then_inc(slot_zeroed, 1)
            gp.wait_ge(prj_out, 16)
            store_stack(gp, 1, ("qh", "ql"))
            gp.wait_ge(slot_zeroed, 1)
            gp.tensor_tensor(w2_parts[1], ffs2, w2_parts[0], ALU.subtract).then_inc(ff_split, 1)
            gp.wait_ge(ff_split, 4)
            half_counts(gp, PAIRS, NP).then_inc(count_done, 1)
            store_stack(gp, 1, ("kh", "kl"))
            for b in range(B):
                gp.wait_ge(stacked[b], 16 * 16)
            gp.wait_ge(count_done, 2)
            zero_rows(0).then_inc(slot_zeroed, 1)

            def tri(ap, blocks):
                return nc.gpsimd.affine_select(out=ap, in_=ap, compare_op=ALU.is_ge, fill=0.0, base=0,
                                               pattern=[[0, blocks], [1, P]], channel_multiplier=-1)

            def squared(it, k):
                gp.wait_ge(sq_done, it * IU + (k + 1))
                gp.sem_inc(pool_turn, 1)

            with gp.Fori(0, NP // PI) as it:
                for k in range(IU):
                    a = A32[k % A_BUFS]
                    kk = k % NU
                    if kk == 0:
                        squared(it, k)
                        gp.tensor_scalar(a, a, 1.0, 0.5, ALU.mult, ALU.add).then_inc(mk_done, 1)
                    elif kk == 3:
                        squared(it, k)
                        tri(a.rearrange("p (b c) -> p b c", b=4)[:, :, 0:P], 4).then_inc(mk_done, 1)
                    elif kk in POOL_LOW:
                        squared(it, k)
                        hi = a.bitcast(BF16).rearrange("p (n two) -> p n two", two=2)[:, :, 1]
                        gp.tensor_tensor(Alo[k % A_BUFS], a, hi, ALU.subtract).then_inc(lo_pool, 1)
                    elif kk in MASKED:
                        squared(it, k)
                        tri(a.rearrange("p (b c) -> p b c", b=2)[:, :, 0:P], 2)
                        tri(a[:, 896:1024].rearrange("p (b c) -> p b c", b=1), 1).then_inc(mk_done, 1)

            def normalise_heads(t, b):
                src = C[:, PAIRS * b:PAIRS * (b + 1), bass.ds(t, 1), :, 0:HD].rearrange("p n a s e -> p (n a) s e")
                zz = zr[:, PAIRS * b:PAIRS * (b + 1), bass.ds(t, 1), :].rearrange("p n a s -> p (n a) s")[:, :, :, None]\
                    .to_broadcast([P, PAIRS, 2, HD])
                gp.tensor_tensor(an[b].rearrange("p (n s) e -> p n s e", s=2), src, zz, ALU.mult).then_inc(an_done, 1)

            gp.wait_ge(z_done, 1)
            for b in range(B):
                normalise_heads(0, b)
            gp.wait_ge(z_done, 2)
            gp.memset(b2s, 0.0).then_inc(b2_zeroed, 1)
            gp.memset(wts, 0.0).then_inc(wts_zeroed, 1)
            with gp.Fori(1, BT) as t:
                for b in range(B):
                    gp.wait_ge(at_ps, t * 2 + (b + 1))
                    gp.sem_inc(pool_turn, 1)
                    normalise_heads(t, b)
            with gp.Fori(0, CH) as c:
                at = acc[:, bass.ds(c * CT, CT), :]
                gp.wait_ge(b2_read, c + 2)
                gp.sem_inc(pool_turn, 1)
                gp.tensor_tensor(at, at, gate[:, bass.ds(c // 2 + 2, 1), :].to_broadcast([P, CT, D]), ALU.mult).then_inc(fstep, 1)
                gp.wait_ge(fstep, c + 1)
                gp.sem_inc(pool_turn, 1)
                gp.tensor_tensor(at, at, xs[:, bass.ds(c * CT, CT), :], ALU.add).then_inc(fin_done, 1)

        @block.scalar
        def _(act):
            act.wait_ge(ld_c, 16)
            nc.scalar.activation(scT[:], cs[:], ACT.Silu).then_inc(silu_done, 1)

            def stddev(k):
                act.wait_ge(var_done, k)
                nc.scalar.activation(rs[:, 1, :], rs[:, 0, :], ACT.Sqrt).then_inc(std_done, 1)

            def hidden_hi(k):
                act.wait_ge(modT_done, 1)
                for c in range(CH):
                    here = hTf[:, 512 * c:512 * c + 512]
                    if c < 2:
                        act.wait_ge(tr_done, CH * k + c + 1)
                        nc.scalar.activation(here, ps[:, 2 + c, :], ACT.Identity, bias=modT[:, 2 * k, 0:1],
                                             scale=modT[:, 2 * k + 1, 0:1]).then_inc(hTf_act, 1)
                        act.wait_ge(hTf_act, 2 * k + c + 1)
                    else:
                        act.wait_ge(hTf_done, 2 * k + c - 1)
                    nc.scalar.activation(hh[:, 512 * c:512 * c + 512], here, ACT.Copy).then_inc(hh_done, 1)

            stddev(1)
            act.wait_ge(ld_wa, 48)
            nc.scalar.activation(wah[:], wst, ACT.Copy).then_inc(wa_hi, 1)
            hidden_hi(0)
            for b in range(B):
                act.wait_ge(scan_done, b + 1)
                nc.scalar.activation(ch[:, N * b:N * b + N], cums[b], ACT.Copy, scale=0.5).then_inc(chi_done, 1)

            act.wait_ge(kenc_zero, 1)
            for b in range(B):
                act.wait_ge(enc_ps, 2 * b + 1)
                for s in range(2):
                    nc.scalar.activation(kenc_sb[:, b, 0, s, :, 64 * s:64 * s + 64],
                                         ps[:, 2 * b, 0:128].rearrange("p (g t) -> p g t", g=2), ACT.Copy).then_inc(enc_hi, 1)
                act.wait_ge(enc_ps, 2 * b + 2)
                for s in range(2):
                    nc.scalar.activation(vencst[64 * s:64 * s + 64, b, :, 0:HD],
                                         ps[64 * s:64 * s + 64, 2 * b + 1, :].rearrange("p (a e) -> p a e", e=HD), ACT.Copy).then_inc(enc_hi, 1)

            act.wait_ge(setup_done, 1)
            act.wait_ge(clo_done, B)
            act.wait_ge(count_done, 1)
            act.sem_inc(prj_c, 2)
            with act.Fori(0, CH) as c:
                for u in range(4):
                    act.wait_ge(prj_ps, c * 4 + (u + 1))
                    nc.scalar.activation(part_at(("qh", "kh")[u // 2], c, u % 2), ps[:, 4 + u, :], ACT.Copy).then_inc(prj_hi, 1)
            act.wait_ge(v_columns, 1)
            for batch in range(B):
                if batch:
                    act.wait_ge(count_done, 2)
                with act.Fori(BT // 4 * batch, BT // 4 * (batch + 1)) as it:
                    for i in range(V_BUFS):
                        for half in range(2):
                            act.wait_ge(v_ps, it * 8 + (2 * i + half + 1))
                            if half == 0:
                                act.wait_ge(v_stored[i], it * 16 + 16)
                            dst = v_st[i][:, 4 * half:4 * half + 4, :, 0:HD]
                            nc.scalar.activation(dst, ps[:, half, :].rearrange("p (a s e) -> p a s e", a=4, s=2),
                                                 ACT.Copy).then_inc(v_hi, 1)
                        for half in range(2):
                            act.wait_ge(c_ps, it * 8 + (2 * i + half + 1))
                            nc.scalar.activation(sums_at(it, i, half),
                                                 ps[:, 2 + half, :].rearrange("p (a s e) -> p a s e", a=4, s=2),
                                                 ACT.Copy).then_inc(prj_c, 1)
            nc.scalar.preload_act_table(ACT.Square)
            with act.Fori(0, NP // PI) as it:
                for k in range(IU):
                    act.wait_ge(s_ready, it * IU + (k + 1))
                    act.wait_ge(av_done, it * IU + (k + 1))
                    nc.scalar.activation(A32[k % A_BUFS], Sb[k % S_BUFS], ACT.Square, bias=sqb[:, 0:1],
                                         scale=SQ_SCALE).then_inc(sq_done, 1)
            act.sem_inc(at_copied, 2)
            with act.Fori(0, BT) as t:
                for b in range(B):
                    act.wait_ge(at_ps, t * 2 + (b + 1) + 2)
                    act.wait_ge(o_ps, t * 2 + (b + 1))
                    nc.scalar.activation(aTh[b].rearrange("p a t -> p (a t)"), ps[:, 2 * b, :].bitcast(BF16), ACT.Copy)
                    nc.scalar.activation(aTl[b].rearrange("p a t -> p (a t)"), ps[:, 2 * b + 1, :].bitcast(F16), ACT.Copy)\
                      .then_inc(at_copied, 1)
            stddev(2)
            hidden_hi(1)
            act.wait_ge(rt, 1)
            nc.scalar.activation(rk.rearrange("p t e -> p (t e)"), rk.rearrange("p t e -> p (t e)"), ACT.Exp).then_inc(exp_done, 1)
            nc.scalar.preload_act_table(ACT.Gelu_apprx_tanh)
            act.wait_ge(ld_k, 16 * 4)
            act.sem_inc(g_ok, PT)
            with act.Fori(0, CH // 2) as it:
                for c in (it * 2, it * 2 + 1):
                    for e in range(E):
                        act.wait_ge(dn_ps, c * E + (e + 1))
                        for pt in range(PT):
                            act.wait_ge(up_ps, c * (E * PT) + (e * PT + pt + 1))
                            nc.scalar.activation(G[e % 2][:, pt, :], ps[:, pt, :], ACT.Gelu_apprx_tanh,
                                                 bias=b1s[:, e, pt:pt + 1]).then_inc(g_ok, 1)

        @block.vector
        def _(v):
            step = [0]

            def link(ins):
                step[0] += 1
                ins.then_inc(chain, 1)
                v.wait_ge(chain, step[0])

            v.wait_ge(ld_hc, 16)
            half_counts(nc.vector, 0, PAIRS).then_inc(count_done, 1)
            v.wait_ge(silu_done, 1)
            nc.vector.tensor_copy(scb, scT[:, :, None].to_broadcast([P, B, P])).then_inc(scb_done, 1)

            def statistics(k):
                if k == 0:
                    for t in range(TILES):
                        if t % CT == 0:
                            v.wait_ge(ld_x[t // CT], 16)
                        nc.vector.bn_stats(stats[:, t, :], xs[:, t, :]).then_inc(st_done, 1)
                for n in range(TILES):
                    t = n if k == 0 else BT * (n % 2) + n // 2
                    v.wait_ge(st_done, TILES * k + n + 1)
                    nc.vector.bn_aggr(mv[:, t, :], stats[:, t, :]).then_inc(agg_done, 1)
                v.wait_ge(agg_done, TILES * (k + 1))
                nc.vector.tensor_scalar(rs[:, 0, :], mv[:, :, 1], LN_EPS, None, ALU.add).then_inc(var_done, 1)
                v.wait_ge(var_done, k + 1)
                v.wait_ge(std_done, k + 1)
                link(nc.vector.reciprocal(rs[:, 2, :], rs[:, 1, :]))
                link(nc.vector.tensor_tensor(rs[:, 3, :], rs[:, 2, :], rs[:, 2, :], ALU.mult))
                link(nc.vector.tensor_tensor(rs[:, 3, :], rs[:, 3, :], rs[:, 0, :], ALU.mult))
                link(nc.vector.tensor_scalar(rs[:, 3, :], rs[:, 3, :], -0.5, 1.5, ALU.mult, ALU.add))
                link(nc.vector.tensor_tensor(rs[:, 2, :], rs[:, 2, :], rs[:, 3, :], ALU.mult))

            def normalise(k, dst):
                for c in range(CH):
                    for t in range(CT * c, CT * (c + 1)):
                        last = nc.vector.tensor_scalar(dst[:, t, :], xs[:, t, :], mv[:, t, 0:1], rs[:, 2, t:t + 1],
                                                       ALU.subtract, ALU.mult)
                    last.then_inc(xn_done, 1)

            def modulate(k):
                for c in (2, 3):
                    v.wait_ge(tr_done, CH * k + c + 1)
                    b = c // 2
                    nc.vector.tensor_scalar(hTf[:, 512 * c:512 * c + 512], ps[:, 2 + c, :],
                                            modT[:, 2 * k + 1, b:b + 1], modT[:, 2 * k, b:b + 1],
                                            ALU.mult, ALU.add).then_inc(hTf_done, 1)

            def hidden_lo(k):
                with v.Fori(0, CH) as c:
                    v.wait_ge(hh_done, CH * k + c + 1)
                    nc.vector.tensor_tensor(hl[:, bass.ds(c * 512, 512)], hTf[:, bass.ds(c * 512, 512)],
                                            hh[:, bass.ds(c * 512, 512)], ALU.subtract).then_inc(hl_done, 1)

            statistics(0)
            normalise(0, xn)
            v.wait_ge(mod_ps, 1)
            nc.vector.tensor_copy(modT[:].rearrange("p m b -> p (m b)"), ps[:, 6, 0:8])
            link(nc.vector.tensor_copy(gate[:].rearrange("p m d -> p (m d)"), ps[:, 7, :]))
            v.sem_inc(mod_out, 1)
            for m in (1, 3):
                last = nc.vector.tensor_scalar(modT[:, m, :], modT[:, m, :], 1.0, None, ALU.add)
            link(last)
            v.sem_inc(modT_done, 1)
            modulate(0)
            hidden_lo(0)
            for b in range(B):
                nc.vector.tensor_tensor_scan(cums[b], hTf[:, N * b:N * b + N], hTf[:, N * b:N * b + N], 0.0,
                                             ALU.add, ALU.bypass).then_inc(scan_done, 1)
            for b in range(B):
                v.wait_ge(chi_done, b + 1)
                nc.vector.scalar_tensor_tensor(out=cl[:, N * b:N * b + N], in0=cums[b], scalar=0.5,
                                               in1=ch[:, N * b:N * b + N], op0=ALU.mult, op1=ALU.subtract).then_inc(clo_done, 1)
            for b in range(B):
                v.wait_ge(enc_hi, 4 * b + 2)
                for s in range(2):
                    last = nc.vector.tensor_tensor(kenc_sb[:, b, 1, s, :, 64 * s:64 * s + 64],
                                                   ps[:, 2 * b, 0:128].rearrange("p (g t) -> p g t", g=2),
                                                   kenc_sb[:, b, 0, s, :, 64 * s:64 * s + 64], ALU.subtract)
                last.then_inc(enc_lo, 1)
                v.wait_ge(enc_hi, 4 * b + 4)
                for s in range(2):
                    last = nc.vector.tensor_tensor(vencst[64 * s:64 * s + 64, b, :, HD + 1:2 * HD + 1],
                                                   ps[64 * s:64 * s + 64, 2 * b + 1, :].rearrange("p (a e) -> p a e", e=HD),
                                                   vencst[64 * s:64 * s + 64, b, :, 0:HD], ALU.subtract)
                last.then_inc(enc_lo, 1)

            v.wait_ge(setup_done, 1)
            with v.Fori(0, CH) as c:
                for u in range(4):
                    v.wait_ge(prj_hi, c * 4 + (u + 1))
                    hi = part_at(("qh", "kh")[u // 2], c, u % 2)
                    lo = part_at(("ql", "kl")[u // 2], c, u % 2)
                    nc.vector.tensor_tensor(lo, ps[:, 4 + u, :], hi, ALU.subtract).then_inc(prj_out, 1)
            v.wait_ge(ff_split, 2)
            for i in range(2):
                nc.vector.memset(v_st[i][:, :, :, HD:HD + 1], 1.0)
                last = nc.vector.memset(v_st[i][:, :, :, VW - 1:VW], 0.0)
            last.then_inc(v_columns, 1)
            v.sem_inc(v_out, 2)
            with v.Fori(0, TILES // 4) as it:
                for i in range(V_BUFS):
                    for half in range(2):
                        v.wait_ge(v_hi, it * 8 + (2 * i + half + 1))
                        pair = v_st[i][:, 4 * half:4 * half + 4]
                        nc.vector.tensor_tensor(pair[:, :, :, HD + 1:2 * HD + 1],
                                                ps[:, half, :].rearrange("p (a s e) -> p a s e", a=4, s=2),
                                                pair[:, :, :, 0:HD], ALU.subtract).then_inc(v_out, 1)
            for b in range(B):
                v.wait_ge(stacked[b], 16 * 16)
            link(nc.vector.tensor_scalar(gtmp, gate[:], 0.0, 2.0, ALU.is_ge, ALU.mult))
            link(nc.vector.scalar_tensor_tensor(out=gate[:], in0=gtmp, scalar=-1.0, in1=gate[:],
                                                op0=ALU.add, op1=ALU.mult))
            link(nc.vector.tensor_scalar(gate[:], gate[:], 0.25, None, ALU.max))
            link(nc.vector.scalar_tensor_tensor(out=gate[:], in0=gtmp, scalar=-1.0, in1=gate[:],
                                                op0=ALU.add, op1=ALU.mult))
            def low(it, k):
                if k % NU in POOL_LOW:
                    return
                if k % NU in MASKED or k % NU == 0:
                    n = sum(1 for j in range(k + 1) if j % NU in MASKED or j % NU == 0)
                    v.wait_ge(mk_done, it * (PI * (len(MASKED) + 1)) + n)
                else:
                    v.wait_ge(sq_done, it * IU + (k + 1))
                a = A32[k % A_BUFS]
                hi = a.bitcast(BF16).rearrange("p (n two) -> p n two", two=2)[:, :, 1]
                nc.vector.tensor_tensor(Alo[k % A_BUFS], a, hi, ALU.subtract).then_inc(lo_done, 1)

            def evacuate(it, k):
                v.wait_ge(av_done, it * IU + (k + 1 + A_BUFS))
                for s, half in DONE_AFTER[k % NU]:
                    acc_c = C[:, bass.ds(it * PI + k // NU, 1), 4 * half:4 * half + 4, s, :].rearrange("p a t e -> p (a t) e")
                    y = ps[:, 4 + 2 * s + half, 0:4 * (HD + 1)].rearrange("p (t e) -> p t e", t=4)
                    nc.vector.tensor_tensor(acc_c, y, acc_c, ALU.add).then_inc(y_free, 1)

            v.sem_inc(y_free, 4)
            with v.Fori(0, NP // PI) as it:
                for k in range(IU):
                    low(it, k)
                    if k >= 2 and (k - 2) % NU in DONE_AFTER:
                        evacuate(it, k - 2)
                evacuate(it, IU - 1)

            v.sem_inc(g_done, 2)
            v.wait_ge(ld_k, 16 * 4)
            link(nc.vector.tensor_copy(wrh[:], wrs[:]))
            nc.vector.tensor_tensor(wrl[:], wrs[:], wrh[:], ALU.subtract)
            v.wait_ge(y_free, 4 * NP + 4)
            nc.vector.tensor_scalar(zr[:], C[:, :, :, :, HD], EPS, None, ALU.add).then_inc(z0, 1)
            v.wait_ge(z0, 1)
            nc.vector.reciprocal(zr[:, :, 0:1], zr[:, :, 0:1]).then_inc(z_done, 1)
            nc.vector.reciprocal(zr[:, :, 1:BT], zr[:, :, 1:BT]).then_inc(z_done, 1)
            def attention_low(t, b):
                v.wait_ge(an_done, t * 2 + (b + 1))
                v.wait_ge(at_ps, t * 2 + (b + 1))
                hi = an[b].bitcast(BF16).rearrange("p h (e two) -> p h e two", two=2)[:, :, :, 1]
                nc.vector.tensor_tensor(anl[b], an[b], hi, ALU.subtract).then_inc(anl_done, 1)

            def row(t, b):
                return xs[:, bass.ds(t + BT * b, 1), :].rearrange("p a d -> p (a d)")

            def gated(t, b):
                v.wait_ge(o_ps, t * 2 + (b + 1) + 2)
                nc.vector.tensor_tensor(tmp[b], ps[:, 4 + b, 0:D], gate[:, b, :], ALU.mult).then_inc(g_done, 1)

            def residual(t, b):
                v.wait_ge(g_done, t * 2 + (b + 1) + 2)
                nc.vector.tensor_tensor(row(t, b), row(t, b), tmp[b], ALU.add).then_inc(x1_done, 1)

            def row_statistics(t, b):
                v.wait_ge(x1_done, t * 2 + (b + 1))
                nc.vector.bn_stats(stats[:, bass.ds(t + BT * b, 1), :].rearrange("p a d -> p (a d)"), row(t, b)).then_inc(st_done, 1)

            nc.vector.tensor_copy(id16, id32[:])
            nc.vector.tensor_copy(idb16, id32[:])
            for b in range(B):
                attention_low(0, b)
            def step_vector(t):
                attention_low(t + 1, 0)
                gated(t, 0)
                attention_low(t + 1, 1)
                residual(t, 0)
                gated(t, 1)
                row_statistics(t, 0)
                residual(t, 1)
                row_statistics(t, 1)

            with v.Fori(0, BT // 2 - 1) as it:
                for j in range(2):
                    step_vector(it * 2 + j)
            step_vector(BT - 2)
            for step_of in (gated, residual, row_statistics):
                for b in range(B):
                    step_of(BT - 1, b)
            statistics(1)
            normalise(1, xn2)
            modulate(1)
            hidden_lo(1)
            v.wait_ge(sc_ps, CH)
            every = lambda ap: ap[:, :, None].to_broadcast([P, TILES, E])
            orders = order[:, None, :].to_broadcast([P, TILES, E])
            link(nc.vector.tensor_tensor(sco, ps[:, 6, 0:TILES * E].rearrange("p (t e) -> p t e", e=E),
                                         brs[:, None, :].to_broadcast([P, TILES, E]), ALU.add))

            def pick(scores, chosen, peak):
                link(nc.vector.tensor_reduce(out=peak, in_=scores, axis=AX.X, op=ALU.max))
                link(nc.vector.tensor_tensor(cand, scores, every(peak), ALU.is_equal))
                link(nc.vector.tensor_tensor(cand, cand, orders, ALU.mult))
                link(nc.vector.tensor_reduce(out=mx[:], in_=cand, axis=AX.X, op=ALU.max))
                link(nc.vector.tensor_tensor(chosen, cand, every(mx[:]), ALU.is_equal))

            pick(sco, best, top[:, 0])
            nc.vector.tensor_tensor(rk, sco, every(top[:, 0]), ALU.subtract).then_inc(rt, 1)
            link(nc.vector.scalar_tensor_tensor(out=sco, in0=best, scalar=-3e38, in1=sco, op0=ALU.mult, op1=ALU.add))
            pick(sco, second, top[:, 1])
            link(nc.vector.tensor_tensor(best, best, second, ALU.add))
            v.wait_ge(exp_done, 1)
            link(nc.vector.tensor_tensor(rk, rk, best, ALU.mult))
            link(nc.vector.tensor_reduce(out=mx[:], in_=rk, axis=AX.X, op=ALU.add))
            link(nc.vector.reciprocal(mx[:], mx[:]))
            v.wait_ge(wts_zeroed, 1)
            nc.vector.tensor_tensor(wts[:, :, 0:E], rk, every(mx[:]), ALU.mult).then_inc(w_ready, 1)
            v.wait_ge(w_ready, 1)
            v.sem_inc(dn_free, 2)
            v.sem_inc(b2_read, 1)
            with v.Fori(0, CH // 2) as it:
                for c in (it * 2, it * 2 + 1):
                    def accumulate(e):
                        v.wait_ge(dn_ps, c * E + (e + 1) + 2)
                        v.wait_ge(dn_free, c * E + (e + 2))
                        for i in range(CT):
                            at = acc[:, bass.ds(c * CT + i, 1), :].rearrange("p a d -> p (a d)")
                            y = ps[:, 4 + e % 2, i * D:(i + 1) * D]
                            weight = wts[:, bass.ds(c * CT + i, 1), e:e + 1].rearrange("p a b -> p (a b)")
                            if e == 0:
                                last = nc.vector.tensor_scalar(at, y, weight, None, ALU.mult)
                            else:
                                last = nc.vector.scalar_tensor_tensor(out=at, in0=y, scalar=weight, in1=at,
                                                                      op0=ALU.mult, op1=ALU.add)
                        last.then_inc(dn_free, 1)

                    for e in range(E):
                        for j in range(2):
                            v.wait_ge(g_ok, c * (E * PT) + (e * PT + 2 * j + 2 + PT))
                            g = G[e % 2][:, 2 * j:2 * j + 2, :]
                            hi = g.bitcast(BF16).rearrange("p a (n two) -> p a n two", two=2)[:, :, :, 1]
                            nc.vector.tensor_tensor(Glo[e % 2][:, 2 * j:2 * j + 2, :], g, hi, ALU.subtract).then_inc(glo, 1)
                        if e == 0:
                            nc.vector.tensor_copy(wc, wts[:, bass.ds(c * CT, CT), :]).then_inc(wc_done, 1)
                        if e == 1:
                            v.wait_ge(wt_ps, c + 1)
                            nc.vector.tensor_copy(wT, ps[:, 6, 0:P]).then_inc(wt_done, 1)
                        if e:
                            accumulate(e - 1)
                    accumulate(E - 1)
                    v.wait_ge(dn_free, c * E + (E + 2))
                    at = acc[:, bass.ds(c * CT, CT), :]
                    v.wait_ge(b2_ps, c + 1)
                    nc.vector.tensor_tensor(at, at, ps[:, 7, :].rearrange("p (i d) -> p i d", d=D), ALU.add).then_inc(b2_read, 1)

        @block.tensor
        def _(pe):
            mm = nc.tensor.matmul

            def three(dst, sh, sl, mh, ml):
                mm(dst, sh, mh, start=True, stop=False)
                mm(dst, sh, ml, start=False, stop=False)
                return mm(dst, sl, mh, start=False, stop=True)

            def router(c):
                pe.wait_ge(hl_done, CH + c + 1)
                for t in range(CT * c, CT * (c + 1)):
                    at = slice(P * t, P * (t + 1))
                    last = three(ps[:, 6, E * t:E * (t + 1)], hh[:, at], hl[:, at], wrh[:], wrl[:])
                last.then_inc(sc_ps, 1)

            def transposes(k, src):
                for c in range(CH):
                    pe.wait_ge(xn_done, CH * k + c + 1)
                    for i in range(CT):
                        last = nc.tensor.transpose(ps[:, 2 + c, i * P:(i + 1) * P], src[:, CT * c + i, :], id32[:])
                    last.then_inc(tr_done, 1)

            pe.wait_ge(ld_wm, 16)
            pe.wait_ge(silu_done, 1)
            for m, col in enumerate((0, 1, 3, 4)):
                mm(ps[:, 6, 2 * m:2 * m + 2], wms[:, col * D:(col + 1) * D], scT[:], start=True, stop=True)
            pe.wait_ge(scb_done, 1)
            for m, col in enumerate((2, 5)):
                for b in range(B):
                    last = mm(ps[:, 7, (2 * m + b) * D:(2 * m + b + 1) * D], scb[:, b, :], wms[:, col * D:(col + 1) * D],
                              start=True, stop=True)
            last.then_inc(mod_ps, 1)
            pe.wait_ge(ld_id, 16)
            transposes(0, xn)

            pe.wait_ge(wa_lo, 1)
            pe.wait_ge(hl_done, CH)
            pe.wait_ge(mod_out, 1)
            for b in range(B):
                t = slice(N * b, N * b + ENC)
                for g in range(2):
                    w = slice(KE0 + P * g, KE0 + P * (g + 1))
                    last = three(ps[:, 2 * b, ENC * g:ENC * (g + 1)], wah[:, w], wal[:, w], hh[:, t], hl[:, t])
                last.then_inc(enc_ps, 1)
                for s in range(2):
                    w = slice(VE0 + 512 * s, VE0 + 512 * (s + 1))
                    last = three(ps[64 * s:64 * s + 64, 2 * b + 1, :], hh[:, t], hl[:, t], wah[:, w], wal[:, w])
                last.then_inc(enc_ps, 1)
            for u in range(4):
                w = Q0 + P * u
                three(ps[:, 4 + u, :], wah[:, w:w + P], wal[:, w:w + P], hh[:, 0:512], hl[:, 0:512]).then_inc(prj_ps, 1)
            with pe.Fori(1, CH) as c:
                for u in range(4):
                    pe.wait_ge(prj_out, c * 4 + (u + 1 - 4))
                    w = Q0 + P * u
                    three(ps[:, 4 + u, :], wah[:, w:w + P], wal[:, w:w + P],
                          hh[:, bass.ds(c * 512, 512)], hl[:, bass.ds(c * 512, 512)]).then_inc(prj_ps, 1)
            pe.wait_ge(clo_done, B)
            pe.wait_ge(enc_lo, 2 * B)
            with pe.Fori(0, TILES // 4) as it:
                for i in range(V_BUFS):
                    for xh, xl, bank0, free, done in ((hh, hl, 0, v_out, v_ps), (ch, cl, 2, prj_c, c_ps)):
                        for half in range(2):
                            w = V0 + 512 * half
                            pe.wait_ge(free, it * 8 + (2 * i + half + 1))
                            three(ps[:, bank0 + half, :], xh[:, bass.ds(it * 4 * P + P * i, P)],
                                  xl[:, bass.ds(it * 4 * P + P * i, P)],
                                  wah[:, w:w + 512], wal[:, w:w + 512]).then_inc(done, 1)
            def scores(it, k):
                hf, unit = (k // NU) % 2, UNITS[k % NU]
                if k % NU == 0:
                    pe.wait_ge(slot[hf], it * (112 * PI // 2) + 112 * (1 + k // (2 * NU)))
                if k >= S_BUFS:
                    pe.wait_ge(sq_done, it * IU + (k + 1 - S_BUFS))
                for off, w, s, j, q0 in unit:
                    col = 2 * N if j == "enc" else N * s + P * j
                    last = mm(Sb[k % S_BUFS][:, off:off + w], kS[hf][:, col:col + P], qS[hf][:, q0:q0 + w], start=True, stop=True)
                last.then_inc(s_ready, 1)

            def products(hf, k, blocks, first):
                a = A32[k % A_BUFS]
                hi = a.bitcast(BF16).rearrange("p (n two) -> p n two", two=2)[:, :, 1]
                for n, (off, s, j, i) in enumerate(blocks):
                    y = ps[:, 4 + 2 * s + i // 4, (i % 4) * (HD + 1):(i % 4 + 1) * (HD + 1)]
                    t = VW * (2 * (BT if j == "enc" else j) + s)
                    vv = vS[hf][:, t:t + VW]
                    one = dict(start=False, stop=True, skip_group_check=True)
                    mm(y, hi[:, off:off + P], vv[:, 0:HD + 1], start=first and n == 0, stop=True, skip_group_check=True)
                    mm(y[:, 0:HD], hi[:, off:off + P], vv[:, HD + 1:2 * HD + 1], **one)
                    last = mm(y, Alo[k % A_BUFS][:, off:off + P], vv[:, 0:HD + 1], **one)
                return last

            def weighted(it, k):
                j, hf, kk = k // NU, k // NU % 2, k % NU
                by_pool = sum(1 for j in range(k + 1) if j % NU in POOL_LOW)
                if kk in POOL_LOW:
                    pe.wait_ge(lo_pool, it * (PI * len(POOL_LOW)) + by_pool)
                else:
                    pe.wait_ge(lo_done, it * (PI * (NU - len(POOL_LOW))) + (k + 1 - by_pool))
                if kk == 0:
                    for n, (s, half) in enumerate(GROUPS[:3]):
                        pe.wait_ge(y_free, it * (4 * PI) + (4 * j + n + 1))
                        products(hf, k, [(512 * half + P * m, s, "enc", 4 * half + m) for m in range(4)], True)
                    return
                blocks = [(off + P * m, s, key, q0 // P + m) for off, w, s, key, q0 in UNITS[kk] for m in range(w // P)]
                last = products(hf, k, blocks, False)
                if kk == 1:
                    s, half = GROUPS[3]
                    pe.wait_ge(y_free, it * (4 * PI) + (4 * j + 4))
                    last = products(hf, k - 1, [(512 * half + P * m, s, "enc", 4 * half + m) for m in range(4)], True)
                last.then_inc(av_done, 2 if kk == 1 else 1)

            pe.wait_ge(prj_c, 2 * TILES + 2)
            pe.wait_ge(v_out, 2 * TILES + 2)
            pe.sem_inc(av_done, A_BUFS)
            for k in range(LAG):
                scores(0, k)
            with pe.Fori(0, NP // PI - 1) as it:
                for k in range(IU):
                    scores(it, k + LAG)
                    weighted(it, k)
            for k in range(IU):
                if k + LAG < IU:
                    scores(NP // PI - 1, k + LAG)
                weighted(NP // PI - 1, k)

            pe.sem_inc(at_ps, 2)
            pe.sem_inc(o_ps, 2)
            def transpose_heads(t, b):
                pe.wait_ge(anl_done, t * 2 + (b + 1))
                pe.wait_ge(at_copied, t * 2 + (b + 1))
                hi = an[b].bitcast(BF16).rearrange("p h (e two) -> p h e two", two=2)[:, :, :, 1]
                for p in range(PAIRS):
                    for src, ident16, bank, dt in ((hi, idb16, 2 * b, BF16), (anl[b], id16, 2 * b + 1, F16)):
                        last = nc.tensor.transpose(ps[:, bank, :].bitcast(dt)[:, P * p:P * (p + 1)],
                                                   src[:, 2 * p:2 * p + 2].rearrange("p s e -> p (s e)"), ident16)
                last.then_inc(at_ps, 1)

            def project(t, b):
                pe.wait_ge(at_copied, t * 2 + (b + 1) + 2)
                pe.wait_ge(g_done, t * 2 + (b + 1))
                bank = ps[:, 4 + b, 0:D]
                for p in range(PAIRS):
                    w = slice(O0 + D * p, O0 + D * (p + 1))
                    mm(bank, aTh[b][:, p, :], wah[:, w], start=p == 0, stop=False)
                    mm(bank, aTh[b][:, p, :], wal[:, w], start=False, stop=False)
                    last = mm(bank, aTl[b][:, p, :], wah[:, w], start=False, stop=p == PAIRS - 1)
                last.then_inc(o_ps, 1)

            transpose_heads(0, 0)
            def step_tensor(t):
                transpose_heads(t, 1)
                project(t, 0)
                transpose_heads(t + 1, 0)
                project(t, 1)

            with pe.Fori(0, BT // 2 - 1) as it:
                for j in range(2):
                    step_tensor(it * 2 + j)
            step_tensor(BT - 2)
            transpose_heads(BT - 1, 1)
            project(BT - 1, 0)
            project(BT - 1, 1)

            pe.wait_ge(ld_k, 16 * 4)
            transposes(1, xn2)
            for c in range(CH):
                router(c)

            pe.wait_ge(ff_split, 4)
            pe.wait_ge(ld_b2, 16 * 4)
            pe.sem_inc(dn_ps, 2)

            with pe.Fori(0, CH // 2) as it:
                for c in (it * 2, it * 2 + 1):
                    def up(e):
                        for pt in range(PT):
                            pe.wait_ge(g_ok, c * (E * PT) + (e * PT + pt + 1))
                            w = slice(P * pt, P * (pt + 1))
                            three(ps[:, pt, :], w1h[:, e, w], w1l[:, e, w], hh[:, bass.ds(c * 512, 512)],
                                  hl[:, bass.ds(c * 512, 512)]).then_inc(up_ps, 1)

                    def down(e):
                        pe.wait_ge(dn_free, c * E + (e + 1))
                        pe.wait_ge(glo, c * (2 * E) + (2 * e + 2))
                        hi = G[e % 2].bitcast(BF16).rearrange("p a (n two) -> p a n two", two=2)[:, :, :, 1]
                        for i in range(CT):
                            bank, t = ps[:, 4 + e % 2, i * D:(i + 1) * D], slice(P * i, P * (i + 1))
                            for pt in range(PT):
                                mm(bank, hi[:, pt, t], w2h[:, e, pt, :], start=pt == 0, stop=False)
                                mm(bank, hi[:, pt, t], w2l[:, e, pt, :], start=False, stop=False)
                                last = mm(bank, Glo[e % 2][:, pt, t], w2h[:, e, pt, :], start=False, stop=pt == PT - 1)
                        last.then_inc(dn_ps, 1)

                    pe.wait_ge(hl_done, c + (CH + 1))
                    up(0)
                    for e in range(1, E):
                        up(e)
                        if e == 1:
                            pe.wait_ge(wc_done, c + 1)
                            nc.tensor.transpose(ps[:, 6, 0:P], wc.rearrange("p t e -> p (t e)"), id32[:]).then_inc(wt_ps, 1)
                        elif e == 2:
                            pe.wait_ge(wt_done, c + 1)
                            pe.wait_ge(b2_read, c + 1)
                            mm(ps[:, 7, :], wT, b2s.rearrange("p i d -> p (i d)"), start=True, stop=True).then_inc(b2_ps, 1)
                        down(e - 1)
                    down(E - 1)


def kernel(L0_attn_x, L0_attn_Wq, L0_attn_Wk, L0_attn_Wv, L0_attn_Wk_enc, L0_attn_Wv_enc, L0_attn_Wout,
           L0_ffn_W1, L0_ffn_b1, L0_ffn_W2, L0_ffn_b2, L0_ffn_Wr, L0_ffn_br, L0_c, L0_wmod):
    import numpy as np
    import concourse.bacc as bacc
    from concourse.bass_utils import run_bass_kernel_spmd

    a = np.asarray

    def groups(w):
        return a(w).reshape(4, 2, 2, FD, D).transpose(4, 1, 2, 0, 3).reshape(D, 256)

    wo = a(L0_attn_Wout).T.reshape(PAIRS, P, D).transpose(1, 0, 2).reshape(P, PAIRS * D)
    ve = a(L0_attn_Wv_enc).reshape(PAIRS, 2, HD, D).transpose(3, 1, 0, 2).reshape(D, H * HD)
    arrays = {
        "x": a(L0_attn_x).reshape(TILES, P, D),
        "wqkT": np.concatenate([groups(L0_attn_Wq), groups(L0_attn_Wk), groups(L0_attn_Wk_enc)], axis=1),
        "wvT": np.concatenate([a(L0_attn_Wv).T, ve], axis=1),
        "woT": wo,
        "w1": a(L0_ffn_W1).transpose(1, 0, 2).reshape(D, E * PF),
        "b1T": a(L0_ffn_b1).reshape(E, PT, P).transpose(2, 0, 1),
        "w2": a(L0_ffn_W2).reshape(E, PT, P, D).transpose(2, 0, 1, 3).reshape(P, E * PT * D),
        "b2": a(L0_ffn_b2),
        "wr": a(L0_ffn_Wr),
        "br": a(L0_ffn_br),
        "cT": a(L0_c).T,
        "wmod": a(L0_wmod),
        "ident": np.eye(P, dtype=np.float32),
        "half_count": (0.5 * (P * np.arange(BT)[None, :] + np.arange(P)[:, None] + 1)).astype(np.float32),
        "index_order": np.broadcast_to(E - np.arange(E, dtype=np.float32), (P, E)),
    }
    nc = bacc.Bacc("TRN2", target_bir_lowering=False, num_devices=1)
    args = {}
    feed = {}
    for name, value in arrays.items():
        feed[name + "_dram"] = np.ascontiguousarray(value)
        args[name] = nc.dram_tensor(name + "_dram", value.shape, F32, kind="ExternalInput").ap()
    out = nc.dram_tensor("out_dram", (TILES, P, D), F32, kind="ExternalOutput").ap()
    adaln_block(nc, out=out, **args)
    r = run_bass_kernel_spmd(nc, [feed], core_ids=[0])
    return r.results[0]["out_dram"].reshape(B, N, D)
```
